# Optimizing a Trainium2 kernel written in Bass

```python
import numpy as np
import jax
import jax.numpy as jnp

def _softmax(x, axis=-1):
    return jax.nn.softmax(x, axis=axis)

def _gelu(x):
    return jax.nn.gelu(x, approximate=True)

def _silu(x):
    return jax.nn.silu(x)

def _sigmoid(x):
    return jax.nn.sigmoid(x)

def _layernorm(x, axis=-1, eps=1e-05):
    m = jnp.mean(x, axis=axis, keepdims=True)
    v = jnp.var(x, axis=axis, keepdims=True)
    return (x - m) / jnp.sqrt(v + eps)

def _scatter_add(tgt, idx, src, axis=0):
    return tgt.at[idx].add(src)

def _segment_sum(src, seg, n):
    return jax.ops.segment_sum(src, seg, n)
kernel_name = 'mk_gnn_preln_d4_gnn_r16_0f3aaf'

def setup_inputs(seed: int=0):
    np.random.seed(seed)
    _w = jnp.asarray

    def _rec_inputs():
        import jax
        import jax.numpy as jnp
        _gk = jax.random.key(seed)
        x = -0.0006008 + 1.001 * jax.random.normal(jax.random.fold_in(_gk, 1), (3125, 128), jnp.float32)
        _s = jax.random.randint(jax.random.fold_in(_gk, 2), (50000,), 0, 3125, jnp.int32)
        _d = jax.random.randint(jax.random.fold_in(_gk, 3), (50000,), 0, 3125, jnp.int32)
        _loop = jnp.arange(3125, dtype=jnp.int32)
        src = jnp.concatenate([_s, _d, _loop])
        dst = jnp.concatenate([_d, _s, _loop])
        _o = jnp.argsort(dst, stable=True)
        src = src[_o]
        dst = dst[_o]
        edge_attr_128 = -6.47781e-05 + 0.999943 * jax.random.normal(jax.random.fold_in(_gk, 13), (103125, 128), jnp.float32)
        return (x, src, dst, edge_attr_128)
    x, src, dst, edge_attr_128 = _rec_inputs()

    def _L0_gnn_setup():
        import jax, jax.numpy as jnp
        import numpy as np
        N = 1250
        E = 12500
        C = 128
        DEPTH = 3
        NEG = -1e+30

        def _lin(key, fan_in, shape):
            b = 1.0 / np.sqrt(fan_in)
            return jax.random.uniform(key, shape, jnp.float32, -b, b)

        def gcn(x, W, b, src, dst, evalid):
            n = x.shape[0]
            h = x @ W
            w = evalid.astype(x.dtype)
            deg = jax.ops.segment_sum(w, dst, num_segments=n) + 1.0
            dinv = jax.lax.rsqrt(deg)
            norm = dinv[src] * dinv[dst] * w
            agg = jax.ops.segment_sum(h[src] * norm[:, None], dst, num_segments=n)
            agg = agg + h * (dinv * dinv)[:, None]
            return agg + b

        def edge_pool(x, src, dst, evalid, wp, bp):
            n = x.shape[0]
            e = (jnp.concatenate([x[src], x[dst]], axis=-1) @ wp)[:, 0] + bp[0]
            e = jnp.where(evalid, e, NEG)
            m = jax.ops.segment_max(e, dst, num_segments=n)
            ex = jnp.exp(e - m[dst])
            s = jax.ops.segment_sum(ex, dst, num_segments=n)
            score = ex / jnp.where(s > 0, s, 1.0)[dst] + 0.5
            order = jnp.argsort(-jnp.where(evalid, score, -jnp.inf))

            def step(state, t):
                avail, cluster, sscore = state
                si, di, sc, ok0 = t
                ok = ok0 & avail[si] & avail[di]
                avail = avail.at[si].set(jnp.where(ok, False, avail[si]))
                avail = avail.at[di].set(jnp.where(ok, False, avail[di]))
                cluster = cluster.at[di].set(jnp.where(ok, si, cluster[di]))
                sscore = sscore.at[si].set(jnp.where(ok, sc, sscore[si]))
                return ((avail, cluster, sscore), None)
            init = (jnp.ones((n,), bool), jnp.arange(n, dtype=src.dtype), jnp.ones((n,), x.dtype))
            (avail, cluster, sscore), _ = jax.lax.scan(step, init, (src[order], dst[order], score[order], evalid[order]))
            new_x = jax.ops.segment_sum(x, cluster, num_segments=n) * sscore[:, None]
            rs, rd = (cluster[src], cluster[dst])
            nontriv = evalid & (rs != rd)
            keyv = jnp.where(nontriv, rs.astype(jnp.int64) * n + rd, jnp.int64(n) * n)
            o2 = jnp.argsort(keyv)
            sk = keyv[o2]
            first = jnp.concatenate([jnp.array([True]), sk[1:] != sk[:-1]]) & (sk < jnp.int64(n) * n)
            new_valid = jnp.zeros((src.shape[0],), bool).at[o2].set(first)
            return (new_x, rs, rd, new_valid, cluster, sscore)

        def _forward(x, src, dst, w_pre, b_pre, w_up, b_up, w_pool, b_pool, w_down, b_down):
            x = x @ w_pre + b_pre
            ev = jnp.ones(src.shape, bool)
            x = jax.nn.relu(gcn(x, w_up[0], b_up[0], src, dst, ev))
            xs = [x]
            edges = [(src, dst, ev)]
            infos = []
            for lvl in range(1, DEPTH + 1):
                x, src, dst, ev, cluster, sscore = edge_pool(x, src, dst, ev, w_pool[lvl - 1], b_pool[lvl - 1])
                x = jax.nn.relu(gcn(x, w_up[lvl], b_up[lvl], src, dst, ev))
                if lvl < DEPTH:
                    xs.append(x)
                    edges.append((src, dst, ev))
                infos.append((cluster, sscore))
            for lvl in reversed(range(DEPTH)):
                cluster, sscore = infos[lvl]
                src, dst, ev = edges[lvl]
                unpooled = (x / sscore[:, None])[cluster]
                x = xs[lvl] + unpooled
                x = gcn(x, w_down[lvl], b_down[lvl], src, dst, ev)
                if lvl > 0:
                    x = jax.nn.relu(x)
            return x
        key = jax.random.key(seed)
        ks = jax.random.split(key, 32)
        x = jax.random.normal(ks[0], (N, C), jnp.float32)
        src = jax.random.randint(ks[1], (E,), 0, N)
        off = jax.random.randint(ks[2], (E,), 1, N)
        dst = (src + off) % N
        inp = {'x': x, 'src': src, 'dst': dst}
        inp['w_pre'] = _lin(ks[3], C, (C, C))
        inp['b_pre'] = jnp.zeros((C,), jnp.float32)
        for i in range(DEPTH + 1):
            inp[f'w_up{i}'] = _lin(ks[4 + i], C, (C, C))
            inp[f'b_up{i}'] = jnp.zeros((C,), jnp.float32)
        for i in range(DEPTH):
            inp[f'w_pool{i}'] = _lin(ks[10 + i], 2 * C, (2 * C, 1))
            inp[f'b_pool{i}'] = jnp.zeros((1,), jnp.float32)
            inp[f'w_down{i}'] = _lin(ks[20 + i], C, (C, C))
            inp[f'b_down{i}'] = jnp.zeros((C,), jnp.float32)
        return inp
    _L0_gnn_all = _L0_gnn_setup()
    _L0_gnn_in = {k: v for k, v in _L0_gnn_all.items() if k in ('w_pre', 'b_pre', 'w_up0', 'b_up0', 'w_up1', 'b_up1', 'w_up2', 'b_up2', 'w_up3', 'b_up3', 'w_pool0', 'b_pool0', 'w_pool1', 'b_pool1', 'w_pool2', 'b_pool2', 'w_down0', 'b_down0', 'w_down1', 'b_down1', 'w_down2', 'b_down2')}
    del _L0_gnn_all

    def _L1_gnn_setup():
        import jax, jax.numpy as jnp
        import numpy as np
        N_NODES = 6250
        N_EDGES = 100000
        D = 128
        NUM_GRAPHS = 16
        IN_FEATURES = 3 * D
        key = jax.random.key(seed)
        ks = jax.random.split(key, 8)
        x = jax.random.normal(ks[0], (N_NODES, D), dtype=jnp.float32)
        edge_attr = jax.random.normal(ks[1], (N_EDGES, D), dtype=jnp.float32)
        u = jax.random.normal(ks[2], (NUM_GRAPHS, D), dtype=jnp.float32)
        edge_index = jax.random.randint(ks[3], (2, N_EDGES), 0, N_NODES, dtype=jnp.int64)
        batch = jnp.sort(jax.random.randint(ks[4], (N_NODES,), 0, NUM_GRAPHS, dtype=jnp.int64))
        W1 = jax.random.normal(ks[5], (IN_FEATURES, D), dtype=jnp.float32) * (1.0 / np.sqrt(IN_FEATURES))
        b1 = jnp.zeros((D,), dtype=jnp.float32)
        W2 = jax.random.normal(ks[6], (D, D), dtype=jnp.float32) * (1.0 / np.sqrt(D))
        b2 = jnp.zeros((D,), dtype=jnp.float32)
        return {'x': x, 'edge_attr': edge_attr, 'u': u, 'W1': W1, 'b1': b1, 'W2': W2, 'b2': b2, 'edge_index': edge_index, 'batch': batch}
    _L1_gnn_all = _L1_gnn_setup()
    _L1_gnn_in = {k: v for k, v in _L1_gnn_all.items() if k in ('u', 'W1', 'b1', 'W2', 'b2')}
    del _L1_gnn_all

    def _L2_gnn_setup():
        import jax, jax.numpy as jnp
        import numpy as np
        N, E, D = (3125, 50000, 128)
        key = jax.random.key(seed)
        ks = jax.random.split(key, 5)
        x = jax.random.normal(ks[0], (N, D), dtype=jnp.float32)
        edge_index = jax.random.randint(ks[1], (2, E), 0, N, dtype=jnp.int64)
        s = 1.0 / np.sqrt(D)
        W_l = jax.random.normal(ks[2], (D, D), dtype=jnp.float32) * s
        b_l = jnp.zeros((D,), dtype=jnp.float32)
        W_r = jax.random.normal(ks[3], (D, D), dtype=jnp.float32) * s
        gamma = jnp.ones((D,), dtype=jnp.float32)
        beta = jnp.zeros((D,), dtype=jnp.float32)
        return {'x': x, 'edge_index': edge_index, 'W_l': W_l, 'b_l': b_l, 'W_r': W_r, 'gamma': gamma, 'beta': beta}
    _L2_gnn_all = _L2_gnn_setup()
    _L2_gnn_in = {k: v for k, v in _L2_gnn_all.items() if k in ('W_l', 'b_l', 'W_r', 'gamma', 'beta')}
    del _L2_gnn_all

    def _L3_gnn_setup():
        import jax, jax.numpy as jnp
        import numpy as np
        N_NODES = 6250
        N_EDGES = 100000
        IN_DIM = 128
        HEADS = 4
        OUT_DIM = 32
        NEG_SLOPE = 0.2
        key = jax.random.key(seed)
        k_x, k_e, k_w, k_as, k_ad = jax.random.split(key, 5)
        x = jax.random.normal(k_x, (N_NODES, IN_DIM), dtype=jnp.float32)
        edge_index = jax.random.randint(k_e, (2, N_EDGES), 0, N_NODES, dtype=jnp.int64)
        W = jax.random.normal(k_w, (IN_DIM, HEADS * OUT_DIM), dtype=jnp.float32) / np.sqrt(IN_DIM)
        att_src = jax.random.normal(k_as, (HEADS, OUT_DIM), dtype=jnp.float32) / np.sqrt(OUT_DIM)
        att_dst = jax.random.normal(k_ad, (HEADS, OUT_DIM), dtype=jnp.float32) / np.sqrt(OUT_DIM)
        bias = jnp.zeros((HEADS * OUT_DIM,), dtype=jnp.float32)
        return {'x': x, 'edge_index': edge_index, 'W': W, 'att_src': att_src, 'att_dst': att_dst, 'bias': bias}
    _L3_gnn_all = _L3_gnn_setup()
    _L3_gnn_in = {k: v for k, v in _L3_gnn_all.items() if k in ('W', 'att_src', 'att_dst', 'bias')}
    del _L3_gnn_all
    return {'x': x, 'src': src, 'dst': dst, 'edge_attr_128': edge_attr_128, 'L0_gnn_w_pre': _L0_gnn_in['w_pre'], 'L0_gnn_b_pre': _L0_gnn_in['b_pre'], 'L0_gnn_w_up0': _L0_gnn_in['w_up0'], 'L0_gnn_b_up0': _L0_gnn_in['b_up0'], 'L0_gnn_w_up1': _L0_gnn_in['w_up1'], 'L0_gnn_b_up1': _L0_gnn_in['b_up1'], 'L0_gnn_w_up2': _L0_gnn_in['w_up2'], 'L0_gnn_b_up2': _L0_gnn_in['b_up2'], 'L0_gnn_w_up3': _L0_gnn_in['w_up3'], 'L0_gnn_b_up3': _L0_gnn_in['b_up3'], 'L0_gnn_w_pool0': _L0_gnn_in['w_pool0'], 'L0_gnn_b_pool0': _L0_gnn_in['b_pool0'], 'L0_gnn_w_pool1': _L0_gnn_in['w_pool1'], 'L0_gnn_b_pool1': _L0_gnn_in['b_pool1'], 'L0_gnn_w_pool2': _L0_gnn_in['w_pool2'], 'L0_gnn_b_pool2': _L0_gnn_in['b_pool2'], 'L0_gnn_w_down0': _L0_gnn_in['w_down0'], 'L0_gnn_b_down0': _L0_gnn_in['b_down0'], 'L0_gnn_w_down1': _L0_gnn_in['w_down1'], 'L0_gnn_b_down1': _L0_gnn_in['b_down1'], 'L0_gnn_w_down2': _L0_gnn_in['w_down2'], 'L0_gnn_b_down2': _L0_gnn_in['b_down2'], 'L1_gnn_u': _L1_gnn_in['u'], 'L1_gnn_W1': _L1_gnn_in['W1'], 'L1_gnn_b1': _L1_gnn_in['b1'], 'L1_gnn_W2': _L1_gnn_in['W2'], 'L1_gnn_b2': _L1_gnn_in['b2'], 'L2_gnn_W_l': _L2_gnn_in['W_l'], 'L2_gnn_b_l': _L2_gnn_in['b_l'], 'L2_gnn_W_r': _L2_gnn_in['W_r'], 'L2_gnn_gamma': _L2_gnn_in['gamma'], 'L2_gnn_beta': _L2_gnn_in['beta'], 'L3_gnn_W': _L3_gnn_in['W'], 'L3_gnn_att_src': _L3_gnn_in['att_src'], 'L3_gnn_att_dst': _L3_gnn_in['att_dst'], 'L3_gnn_bias': _L3_gnn_in['bias']}

def reference(x, src, dst, edge_attr_128, L0_gnn_w_pre, L0_gnn_b_pre, L0_gnn_w_up0, L0_gnn_b_up0, L0_gnn_w_up1, L0_gnn_b_up1, L0_gnn_w_up2, L0_gnn_b_up2, L0_gnn_w_up3, L0_gnn_b_up3, L0_gnn_w_pool0, L0_gnn_b_pool0, L0_gnn_w_pool1, L0_gnn_b_pool1, L0_gnn_w_pool2, L0_gnn_b_pool2, L0_gnn_w_down0, L0_gnn_b_down0, L0_gnn_w_down1, L0_gnn_b_down1, L0_gnn_w_down2, L0_gnn_b_down2, L1_gnn_u, L1_gnn_W1, L1_gnn_b1, L1_gnn_W2, L1_gnn_b2, L2_gnn_W_l, L2_gnn_b_l, L2_gnn_W_r, L2_gnn_gamma, L2_gnn_beta, L3_gnn_W, L3_gnn_att_src, L3_gnn_att_dst, L3_gnn_bias):
    import jax
    import jax.numpy as jnp

    def _L0_gnn_ref(x, src, dst, w_pre, b_pre, w_up0, b_up0, w_up1, b_up1, w_up2, b_up2, w_up3, b_up3, w_pool0, b_pool0, w_pool1, b_pool1, w_pool2, b_pool2, w_down0, b_down0, w_down1, b_down1, w_down2, b_down2):
        import jax, jax.numpy as jnp
        import numpy as np
        N = 1250
        E = 12500
        C = 128
        DEPTH = 3
        NEG = -1e+30

        def _lin(key, fan_in, shape):
            b = 1.0 / np.sqrt(fan_in)
            return jax.random.uniform(key, shape, jnp.float32, -b, b)

        def gcn(x, W, b, src, dst, evalid):
            n = x.shape[0]
            h = x @ W
            w = evalid.astype(x.dtype)
            deg = jax.ops.segment_sum(w, dst, num_segments=n) + 1.0
            dinv = jax.lax.rsqrt(deg)
            norm = dinv[src] * dinv[dst] * w
            agg = jax.ops.segment_sum(h[src] * norm[:, None], dst, num_segments=n)
            agg = agg + h * (dinv * dinv)[:, None]
            return agg + b

        def edge_pool(x, src, dst, evalid, wp, bp):
            n = x.shape[0]
            e = (jnp.concatenate([x[src], x[dst]], axis=-1) @ wp)[:, 0] + bp[0]
            e = jnp.where(evalid, e, NEG)
            m = jax.ops.segment_max(e, dst, num_segments=n)
            ex = jnp.exp(e - m[dst])
            s = jax.ops.segment_sum(ex, dst, num_segments=n)
            score = ex / jnp.where(s > 0, s, 1.0)[dst] + 0.5
            order = jnp.argsort(-jnp.where(evalid, score, -jnp.inf))

            def step(state, t):
                avail, cluster, sscore = state
                si, di, sc, ok0 = t
                ok = ok0 & avail[si] & avail[di]
                avail = avail.at[si].set(jnp.where(ok, False, avail[si]))
                avail = avail.at[di].set(jnp.where(ok, False, avail[di]))
                cluster = cluster.at[di].set(jnp.where(ok, si, cluster[di]))
                sscore = sscore.at[si].set(jnp.where(ok, sc, sscore[si]))
                return ((avail, cluster, sscore), None)
            init = (jnp.ones((n,), bool), jnp.arange(n, dtype=src.dtype), jnp.ones((n,), x.dtype))
            (avail, cluster, sscore), _ = jax.lax.scan(step, init, (src[order], dst[order], score[order], evalid[order]))
            new_x = jax.ops.segment_sum(x, cluster, num_segments=n) * sscore[:, None]
            rs, rd = (cluster[src], cluster[dst])
            nontriv = evalid & (rs != rd)
            keyv = jnp.where(nontriv, rs.astype(jnp.int64) * n + rd, jnp.int64(n) * n)
            o2 = jnp.argsort(keyv)
            sk = keyv[o2]
            first = jnp.concatenate([jnp.array([True]), sk[1:] != sk[:-1]]) & (sk < jnp.int64(n) * n)
            new_valid = jnp.zeros((src.shape[0],), bool).at[o2].set(first)
            return (new_x, rs, rd, new_valid, cluster, sscore)

        def _forward(x, src, dst, w_pre, b_pre, w_up, b_up, w_pool, b_pool, w_down, b_down):
            x = x @ w_pre + b_pre
            ev = jnp.ones(src.shape, bool)
            x = jax.nn.relu(gcn(x, w_up[0], b_up[0], src, dst, ev))
            xs = [x]
            edges = [(src, dst, ev)]
            infos = []
            for lvl in range(1, DEPTH + 1):
                x, src, dst, ev, cluster, sscore = edge_pool(x, src, dst, ev, w_pool[lvl - 1], b_pool[lvl - 1])
                x = jax.nn.relu(gcn(x, w_up[lvl], b_up[lvl], src, dst, ev))
                if lvl < DEPTH:
                    xs.append(x)
                    edges.append((src, dst, ev))
                infos.append((cluster, sscore))
            for lvl in reversed(range(DEPTH)):
                cluster, sscore = infos[lvl]
                src, dst, ev = edges[lvl]
                unpooled = (x / sscore[:, None])[cluster]
                x = xs[lvl] + unpooled
                x = gcn(x, w_down[lvl], b_down[lvl], src, dst, ev)
                if lvl > 0:
                    x = jax.nn.relu(x)
            return x
        w_up = [w_up0, w_up1, w_up2, w_up3]
        b_up = [b_up0, b_up1, b_up2, b_up3]
        w_pool = [w_pool0, w_pool1, w_pool2]
        b_pool = [b_pool0, b_pool1, b_pool2]
        w_down = [w_down0, w_down1, w_down2]
        b_down = [b_down0, b_down1, b_down2]
        return _forward(x, src, dst, w_pre, b_pre, w_up, b_up, w_pool, b_pool, w_down, b_down)

    def _L1_gnn_ref(x, edge_attr, u, W1, b1, W2, b2, edge_index, batch):
        import jax, jax.numpy as jnp
        import numpy as np
        N_NODES = 6250
        N_EDGES = 100000
        D = 128
        NUM_GRAPHS = 16
        IN_FEATURES = 3 * D
        n_nodes = x.shape[0]
        dest = edge_index[1]
        summed = jax.ops.segment_sum(edge_attr, dest, num_segments=n_nodes)
        counts = jax.ops.segment_sum(jnp.ones((edge_attr.shape[0],), dtype=edge_attr.dtype), dest, num_segments=n_nodes)
        agg_edges = summed / jnp.maximum(counts, 1.0)[:, None]
        feats = jnp.concatenate([x, agg_edges, u[batch]], axis=1)
        h = jax.nn.relu(feats @ W1 + b1)
        return h @ W2 + b2

    def _L2_gnn_ref(x, edge_index, W_l, b_l, W_r, gamma, beta):
        import jax, jax.numpy as jnp
        import numpy as np
        N, E, D = (3125, 50000, 128)
        src = edge_index[0]
        dst = edge_index[1]
        n = x.shape[0]
        summed = jax.ops.segment_sum(x[src], dst, num_segments=n)
        cnt = jax.ops.segment_sum(jnp.ones((src.shape[0],), x.dtype), dst, num_segments=n)
        mean_nbr = summed / jnp.maximum(cnt, 1.0)[:, None]
        h = mean_nbr @ W_l.T + b_l + x @ W_r.T
        mu = jnp.mean(h, axis=-1, keepdims=True)
        var = jnp.mean(jnp.square(h - mu), axis=-1, keepdims=True)
        h = (h - mu) * jax.lax.rsqrt(var + 1e-05) * gamma + beta
        h = jax.nn.relu(h)
        return h + x

    def _L3_gnn_ref(x, edge_index, W, att_src, att_dst, bias):
        import jax, jax.numpy as jnp
        import numpy as np
        N_NODES = 6250
        N_EDGES = 100000
        IN_DIM = 128
        HEADS = 4
        OUT_DIM = 32
        NEG_SLOPE = 0.2
        N = x.shape[0]
        H, D = att_src.shape
        loop = jnp.arange(N, dtype=edge_index.dtype)
        src = jnp.concatenate([edge_index[0], loop])
        dst = jnp.concatenate([edge_index[1], loop])
        h = (x @ W).reshape(N, H, D)
        a_src = jnp.einsum('nhd,hd->nh', h, att_src)
        a_dst = jnp.einsum('nhd,hd->nh', h, att_dst)
        e = jax.nn.leaky_relu(a_src[src] + a_dst[dst], NEG_SLOPE)
        e_max = jax.ops.segment_max(e, dst, num_segments=N)
        e_max = jnp.where(jnp.isfinite(e_max), e_max, jnp.float32(0))
        ex = jnp.exp(e - e_max[dst])
        denom = jax.ops.segment_sum(ex, dst, num_segments=N)
        alpha = ex / (denom[dst] + jnp.float32(1e-16))
        msg = h[src] * alpha[:, :, None]
        out = jax.ops.segment_sum(msg, dst, num_segments=N)
        out = out.reshape(N, H * D) + bias
        return jax.nn.elu(out)
    edge_index = jnp.stack([src, dst])
    batch0 = jnp.zeros((3125,), jnp.int32)
    h = jnp.maximum(_layernorm(x, axis=-1), 0.0)
    x = x + _L0_gnn_ref(h, src, dst, L0_gnn_w_pre, L0_gnn_b_pre, L0_gnn_w_up0, L0_gnn_b_up0, L0_gnn_w_up1, L0_gnn_b_up1, L0_gnn_w_up2, L0_gnn_b_up2, L0_gnn_w_up3, L0_gnn_b_up3, L0_gnn_w_pool0, L0_gnn_b_pool0, L0_gnn_w_pool1, L0_gnn_b_pool1, L0_gnn_w_pool2, L0_gnn_b_pool2, L0_gnn_w_down0, L0_gnn_b_down0, L0_gnn_w_down1, L0_gnn_b_down1, L0_gnn_w_down2, L0_gnn_b_down2)
    h = jnp.maximum(_layernorm(x, axis=-1), 0.0)
    x = x + _L1_gnn_ref(h, edge_attr_128, L1_gnn_u, L1_gnn_W1, L1_gnn_b1, L1_gnn_W2, L1_gnn_b2, edge_index, batch0)
    h = jnp.maximum(_layernorm(x, axis=-1), 0.0)
    x = x + _L2_gnn_ref(h, edge_index, L2_gnn_W_l, L2_gnn_b_l, L2_gnn_W_r, L2_gnn_gamma, L2_gnn_beta)
    h = jnp.maximum(_layernorm(x, axis=-1), 0.0)
    x = x + _L3_gnn_ref(h, edge_index, L3_gnn_W, L3_gnn_att_src, L3_gnn_att_dst, L3_gnn_bias)
    return x

_drawn_inputs = setup_inputs


def setup_inputs(seed=0):
    import zlib

    import numpy as np

    out = dict(_drawn_inputs(seed))
    spreads = {'L0_gnn_b_pre': (0.0, 0.424),
     'L0_gnn_b_up0': (0.0, 0.1),
     'L0_gnn_b_up1': (0.0, 0.409),
     'L0_gnn_b_up2': (0.0, 0.348),
     'L0_gnn_b_up3': (0.0, 0.1),
     'L0_gnn_b_down0': (0.0, 0.1),
     'L0_gnn_b_down1': (0.0, 0.1),
     'L0_gnn_b_down2': (0.0, 0.1),
     'L1_gnn_b1': (0.0, 0.1),
     'L1_gnn_b2': (0.0, 0.1),
     'L2_gnn_b_l': (0.0, 0.1),
     'L2_gnn_gamma': (1.0, 0.2),
     'L2_gnn_beta': (0.0, 0.1),
     'L3_gnn_bias': (0.0, 0.1)}
    factors = {'L0_gnn_w_up2': 3.228,
     'L0_gnn_w_up3': 2.992,
     'L0_gnn_w_pool0': 8.0,
     'L0_gnn_w_pool1': 8.0,
     'L0_gnn_w_pool2': 8.0,
     'L3_gnn_att_dst': 6.364}
    for name, (base, spread) in spreads.items():
        noise = np.random.default_rng([zlib.crc32(name.encode()), seed]).standard_normal(out[name].shape)
        drawn = base * np.exp(spread * noise) if base else spread * noise
        out[name] = jnp.asarray(drawn.astype(out[name].dtype))
    for name, factor in factors.items():
        out[name] = (out[name] * factor).astype(out[name].dtype)
    return out
```

```python
import numpy as np
import concourse.bass as bass
from concourse import mybir
from contextlib import ExitStack, contextmanager

F32 = mybir.dt.float32
BF16 = mybir.dt.bfloat16
F8 = mybir.dt.float8e4
I32 = mybir.dt.int32
I16 = mybir.dt.int16
ALU = mybir.AluOpType
ACT = mybir.ActivationFunctionType
AX = mybir.AxisListType

N = 3125
E = 103125
C = 128
P = 128
T = -(-N // P)
NP = T * P
ZERO = NP
CH = 2 * (-(-E // P) // 2 + 1)
G = 125
K = N // G
DEPTH = 3
EXP0 = 251
NEG = -1e30
FAR = -2e38
SHUT = 1e38
HEADS, HD = 4, 32
PB = 512


class Ctx:

    def __init__(self, nc, ios):
        self.nc, self.ins = nc, ios


class Buffers:

    def __init__(self, nc, tag, ctx):
        self.nc, self.tag, self.ctx, self.sems = nc, tag, ctx, []

    def sb(self, name, shape, dt):
        return self.ctx.enter_context(self.nc.sbuf_tensor(f"{self.tag}_{name}", shape, dt))

    def ps(self, name, shape, dt=F32):
        return self.ctx.enter_context(self.nc.psum_tensor(f"{self.tag}_{name}", shape, dt))

    def sem(self, name):
        self.sems.append(self.nc.alloc_semaphore(f"{self.tag}_{name}"))
        return self.sems[-1]

    def block(self):
        return self.ctx.enter_context(self.nc.Block())


@contextmanager
def Phase(nc, tag):
    with ExitStack() as ctx:
        f = Buffers(nc, tag, ctx)
        yield f
    if f.sems:
        nc.clear_and_free_semaphores(f.sems)
        nc.all_engine_barrier()


def nodes(dram):
    return dram[0:NP, :].rearrange("(t p) c -> p t c", p=P)


def load_constants(k):
    nc = k.nc
    with Phase(nc, "const") as f:
        loaded = f.sem("loaded")
        zeroed = f.sem("zeroed")
        cast = f.sem("cast")
        wrote = f.sem("wrote")
        zrow = f.sb("zrow", [1, NP], BF16)
        b = f.block()

        @b.sync
        def _(sp):
            sp.dma_start(k.ident[:, :], k.ins["c_ident"]).then_inc(loaded, 16)
            sp.dma_start(k.small[:, :], k.ins["c_small"]).then_inc(loaded, 16)
            sp.wait_ge(zeroed, 1)
            for m in (*k.Drow, k.RT):
                sp.dma_start(m[ZERO:ZERO + 1, :], zrow[0:1, :]).then_inc(wrote, 16)
            sp.dma_start(k.Xg[ZERO:ZERO + 1, :], zrow[0:1, 0:2 * C].bitcast(F32)).then_inc(wrote, 16)
            sp.wait_ge(wrote, 16 * (len(k.Drow) + 2))

        @b.vector
        def _(v):
            v.memset(zrow[:, :], 0.0).then_inc(zeroed, 1)
            v.memset(k.ones[:, :], 1.0)
            v.wait_ge(loaded, 32)
            v.tensor_copy(k.identb[:, :], k.ident[:, :]).then_inc(cast, 1)
            v.wait_ge(cast, 1)


def build_counts(k):
    nc = k.nc
    with Phase(nc, "edges") as f:
        dst = f.sb("dst", [P, CH], F32)
        src = f.sb("src", [P, CH], F32)
        first = f.sb("first", [P, T], I32)
        pairs = f.sb("pairs", [P, T], I32)
        with Phase(nc, "bounds") as g:
            loaded, below, summed, done = g.sem("loaded"), g.sem("below"), g.sem("summed"), g.sem("done")
            raw = g.sb("raw", [P, 2, CH], I32)
            hits = g.sb("hits", [P, CH], F32)
            cnt = g.sb("cnt", [P, T + 1], F32)
            cntf = g.sb("cntf", [P, T + 1], F32)
            cnti = g.sb("cnti", [P, T + 1], I32)
            tot = g.ps("tot", [P, PB])
            b = g.block()

            @b.sync
            def _(sp):
                sp.dma_start(raw[:, 0, :], k.ins["dst_T"]).then_inc(loaded, 16)
                sp.dma_start(raw[:, 1, :], k.ins["src_T"]).then_inc(loaded, 16)

            @b.vector
            def _(v):
                v.wait_ge(loaded, 32)
                v.tensor_copy(dst[:, :], raw[:, 0, :])
                v.tensor_copy(src[:, :], raw[:, 1, :])
                v.drain()
                for t in range(T + 1):
                    v.tensor_scalar(hits[:, :], dst[:, :], float(t * P), 0.0, ALU.is_lt, ALU.add,
                                    accum_out=cnt[:, t:t + 1])
                    v.drain()
                v.sem_inc(below, 1)
                v.wait_ge(summed, 1)
                v.tensor_copy(cntf[:, :], tot[:, 0:T + 1])
                v.drain()
                v.tensor_copy(cnti[:, :], cntf[:, :])
                v.drain()
                v.tensor_scalar(cnti[:, :], cnti[:, :], 7, None, ALU.arith_shift_right)
                v.drain()
                v.tensor_copy(first[:, :], cnti[:, 0:T])
                v.tensor_tensor(pairs[:, :], cnti[:, 1:T + 1], cnti[:, 0:T], ALU.subtract)
                v.drain()
                v.tensor_scalar(pairs[:, :], pairs[:, :], 2.0, None, ALU.add)
                v.drain()
                v.tensor_scalar(pairs[:, :], pairs[:, :], 1, None, ALU.arith_shift_right).then_inc(done, 1)
                v.wait_ge(done, 1)

            @b.tensor
            def _(pe):
                pe.wait_ge(below, 1)
                nc.tensor.matmul(tot[:, 0:T + 1], k.ones[:, 0:P], cnt[:, :], start=True, stop=True).then_inc(summed, 1)

        s_attr = [f.sem("attr0"), f.sem("attr1")]
        s_oh, s_mm, s_zero = [f.sem("oh0"), f.sem("oh1")], [f.sem("mm0"), f.sem("mm1")], f.sem("zeroed")
        s_open, s_full, s_row, s_tr, s_blk, s_wr = f.sem("open"), f.sem("full"), f.sem("row"), f.sem("tr"), f.sem("blk"), f.sem("wr")
        attr = f.sb("attr", [P, 2, C], F32)
        zb = f.sb("zb", [P, PB], BF16)
        iota = f.sb("iota", [P, NP], I16)
        ohd = [f.sb(f"ohd{u}", [P, P], F32) for u in range(2)]
        ohdb = [f.sb(f"ohdb{u}", [P, P], BF16) for u in range(2)]
        ohs = [f.sb(f"ohs{u}", [P, NP], BF16) for u in range(2)]
        dloc = f.sb("dloc", [P, CH], F32)
        row = f.sb("row", [P, NP], BF16)
        blk = f.sb("blk", [P, T, P], BF16)
        mean = f.sb("mean", [P, C], F32)
        icnt = f.sb("icnt", [P, 1], F32)
        acc = f.ps("acc", [P, 8 * PB])
        accb = acc[:, :].bitcast(BF16)
        banks = [(j * PB, min(NP, (j + 1) * PB)) for j in range(-(-NP // PB))]
        AT = 7 * PB
        s_iota = f.sem("iota")
        b = f.block()

        @b.sync
        def _(sp):
            sp.dma_start(iota[:, :], k.ins["c_iota"]).then_inc(s_iota, 16)
            step = sp.alloc_register("step")
            sp.reg_mov(step, 0)
            for t in range(T):
                c0 = sp.value_load(first[0:1, t:t + 1], min_val=0, max_val=CH - 2)
                n = sp.value_load(pairs[0:1, t:t + 1], min_val=1, max_val=CH // 2)
                with sp.Fori(0, n) as i:
                    g = sp.snap(step)
                    for u in range(2):
                        sp.wait_ge(s_mm[u], g + 1)
                        c = sp.snap(c0 + i * 2 + u).with_bounds(min_val=0, max_val=CH - 1)
                        sp.dma_start(attr[:, u, :], k.ins["edge_attr"].rearrange("(c p) n -> c p n", p=P)[bass.ds(c, 1), :, :].rearrange("a p n -> (a p) n")).then_inc(s_attr[u], 16)
                    sp.reg_add(step, step, 1)
                sp.wait_ge(s_row, 3 * (t + 1))
                sp.dma_start(k.Drow[0][t * P:(t + 1) * P, :], row[:, :]).then_inc(s_wr, 16)
                sp.dma_start(k.mean[t * P:(t + 1) * P, :], mean[:, :]).then_inc(s_wr, 16)
                sp.wait_ge(s_blk, 2 * (t + 1))
                sp.dma_start(k.TB[0][t], blk[:, :, :]).then_inc(s_wr, 16)
            sp.wait_ge(s_wr, 48 * T)

        @b.vector
        def _(v):
            v.memset(zb[:, :], 0.0).then_inc(s_zero, 1)
            v.wait_ge(s_iota, 16)
            step = v.alloc_register("step")
            v.reg_mov(step, 0)
            for t in range(T):
                v.tensor_scalar(dloc[:, :], dst[:, :], float(-t * P), None, ALU.add)
                v.drain()
                c0 = v.value_load(first[0:1, t:t + 1], min_val=0, max_val=CH - 2)
                n = v.value_load(pairs[0:1, t:t + 1], min_val=1, max_val=CH // 2)
                with v.Fori(0, n) as i:
                    g = v.snap(step)
                    for u in range(2):
                        c = v.snap(c0 + i * 2 + u).with_bounds(min_val=0, max_val=CH - 1)
                        v.wait_ge(s_mm[u], g + 1)
                        v.tensor_scalar(ohd[u][:, :], iota[:, 0:P], dloc[:, bass.ds(c, 1)], None, ALU.is_equal).then_inc(s_oh[u], 1)
                        v.tensor_scalar(ohdb[u][:, :], iota[:, 0:P], dloc[:, bass.ds(c, 1)], None, ALU.is_equal).then_inc(s_oh[u], 1)
                        v.tensor_scalar(ohs[u][:, :], iota[:, :], src[:, bass.ds(c, 1)], None, ALU.is_equal).then_inc(s_oh[u], 1)
                    v.reg_add(step, step, 1)
                v.wait_ge(s_full, t + 1)
                if t:
                    v.wait_ge(s_wr, 48 * t)
                v.tensor_scalar(row[:, :], acc[:, 0:NP], 1.0, 0.0, ALU.mult, ALU.add,
                                accum_out=k.count[:, t:t + 1]).then_inc(s_row, 1)
                v.drain()
                v.tensor_scalar(icnt[:, :], k.count[:, t:t + 1], 1.0, None, ALU.max)
                v.drain()
                v.reciprocal(icnt[:, :], icnt[:, :]).then_inc(s_row, 1)
                v.drain()
                v.tensor_scalar(mean[:, :], acc[:, AT:AT + C], icnt[:, 0:1], None, ALU.mult).then_inc(s_row, 1)
                v.tensor_scalar(k.D[:, t, :], row[:, :], 1.0, None, ALU.min, saturate=False)
                v.wait_ge(s_tr, t + 1)
                v.tensor_copy(blk[:, :, :].rearrange("p t n -> p (t n)"), accb[:, 0:NP]).then_inc(s_blk, 1)
                v.drain()
                v.tensor_scalar(k.Tm[:, :, t * P:(t + 1) * P], blk[:, :, :], 1.0, None, ALU.min, saturate=False).then_inc(s_blk, 1)

        @b.tensor
        def _(pe):
            pe.wait_ge(s_zero, 1)
            for u in range(2):
                pe.sem_inc(s_mm[u], 1)
            step = pe.alloc_register("step")
            pe.reg_mov(step, 0)
            for t in range(T):
                if t:
                    pe.wait_ge(s_blk, 2 * t)
                for j in range(8):
                    nc.tensor.matmul(acc[:, j * PB:(j + 1) * PB], zb[:, 0:P], zb[:, :], start=True, stop=True)
                n = pe.value_load(pairs[0:1, t:t + 1], min_val=1, max_val=CH // 2)
                with pe.Fori(0, n) as i:
                    g = pe.snap(step)
                    for u in range(2):
                        pe.wait_ge(s_oh[u], g * 3 + 3)
                        for lo, hi in banks:
                            nc.tensor.matmul(acc[:, lo:hi], ohdb[u][:, :], ohs[u][:, lo:hi], start=False, stop=True, skip_group_check=True)
                        pe.wait_ge(s_attr[u], g * 16 + 16)
                        nc.tensor.matmul(acc[:, AT:AT + C], ohd[u][:, :], attr[:, u, :], start=False, stop=True, skip_group_check=True).then_inc(s_mm[u], 1)
                    pe.reg_add(step, step, 1)
                pe.drain()
                pe.sem_inc(s_full, 1)
                pe.wait_ge(s_row, 3 * (t + 1))
                for j in range(T):
                    m = nc.tensor.transpose(accb[:, j * P:(j + 1) * P], row[:, j * P:(j + 1) * P], k.identb[:, :])
                m.then_inc(s_tr, 1)


def normalise(k, tag, xin, out, add=None, keep=None):
    nc = k.nc
    with Phase(nc, tag) as f:
        x, sq = f.sb("x", [P, T, C], F32), f.sb("sq", [P, T, C], F32)
        mu, var, eps = f.sb("mu", [P, T], F32), f.sb("var", [P, T], F32), f.sb("eps", [P, 1], F32)
        loaded, s_var, s_std, s_done, s_sum, wrote = f.sem("in"), f.sem("var"), f.sem("std"), f.sem("done"), f.sem("sum"), f.sem("wr")
        b = f.block()

        @b.sync
        def _(sp):
            sp.dma_start(x[:, :, :], nodes(xin)).then_inc(loaded, 16)
            if add is not None:
                sp.dma_start(sq[:, :, :], nodes(add)).then_inc(loaded, 16)
                sp.wait_ge(s_sum, 1)
                sp.dma_start(nodes(keep), x[:, :, :]).then_inc(wrote, 16)
                sp.wait_ge(wrote, 16)
                sp.sem_inc(s_sum, 1)
            sp.wait_ge(s_done, 1)
            sp.dma_start(nodes(out), sq[:, :, :]).then_inc(wrote, 16)
            sp.wait_ge(wrote, 16 if add is None else 32)

        @b.vector
        def _(v):
            v.memset(eps[:, :], 1e-5)
            v.wait_ge(loaded, 16 if add is None else 32)
            if add is not None:
                v.tensor_tensor(x[:, :, :], x[:, :, :], sq[:, :, :], ALU.add).then_inc(s_sum, 1)
                v.wait_ge(s_sum, 2)
            v.tensor_reduce(mu[:, :], x[:, :, :], AX.X, ALU.add)
            v.drain()
            v.tensor_scalar(mu[:, :], mu[:, :], 1.0 / C, None, ALU.mult)
            v.drain()
            v.tensor_tensor(x[:, :, :], x[:, :, :], mu[:, :].unsqueeze(2).to_broadcast([P, T, C]), ALU.subtract)
            v.drain()
            v.tensor_tensor(sq[:, :, :], x[:, :, :], x[:, :, :], ALU.mult)
            v.drain()
            v.tensor_reduce(var[:, :], sq[:, :, :], AX.X, ALU.add).then_inc(s_var, 1)
            v.wait_ge(s_std, 1)
            v.reciprocal(var[:, :], mu[:, :])
            v.drain()
            v.tensor_tensor(sq[:, :, :], x[:, :, :], var[:, :].unsqueeze(2).to_broadcast([P, T, C]), ALU.mult)
            v.drain()
            v.tensor_scalar(sq[:, :, :], sq[:, :, :], 0.0, None, ALU.max).then_inc(s_done, 1)

        @b.scalar
        def _(a):
            a.wait_ge(s_var, 1)
            nc.scalar.activation(mu[:, :], var[:, :], ACT.Sqrt, bias=eps[:, 0:1], scale=1.0 / C).then_inc(s_std, 1)


def project(k, tag, ins, bias, out, relu=False, shared=None, residual=None):
    nc = k.nc
    with Phase(nc, tag) as f:
        n = len(ins)
        xs = [f.sb(f"x{i}", [P, T, C], F32) for i in range(n)]
        ws = [f.sb(f"w{i}", [C, C], F32) for i in range(n)]
        br, bb, xt = f.sb("br", [1, C], F32), f.sb("bb", [P, C], F32), f.sb("xt", [P, 2, C], F32)
        ucol, ub, wu = f.sb("ucol", [C, 1], F32), f.sb("ub", [C, P], F32), f.sb("wu", [C, C], F32)
        res = f.sb("res", [P, T, C], F32) if residual is not None else None
        pt, ph, pb = [f.ps(f"pt{i}", [P, PB]) for i in range(2)], [f.ps(f"ph{i}", [P, PB]) for i in range(2)], f.ps("pb", [P, PB])
        loaded, s_u, s_b, s_bb, s_t, s_c, s_h, s_o, wrote = [f.sem(x) for x in ("in", "u", "b", "bb", "t", "c", "h", "o", "wr")]
        loads = 2 * n + (bias is not None) + (2 if shared else 0) + (residual is not None)
        b = f.block()

        @b.sync
        def _(sp):
            for i, (x, w) in enumerate(ins):
                sp.dma_start(xs[i][:, :, :], nodes(x)).then_inc(loaded, 16)
                sp.dma_start(ws[i][:, :], w).then_inc(loaded, 16)
            if bias is not None:
                sp.dma_start(br[:, :], bias.rearrange("(a n) -> a n", a=1)).then_inc(loaded, 16)
            if shared:
                sp.dma_start(ucol[:, :], shared[0].rearrange("(n a) -> n a", a=1)).then_inc(loaded, 16)
                sp.dma_start(wu[:, :], shared[1]).then_inc(loaded, 16)
            if residual is not None:
                sp.dma_start(res[:, :, :], nodes(residual)).then_inc(loaded, 16)
            sp.wait_ge(s_o, T)
            sp.dma_start(nodes(out), xs[0][:, :, :]).then_inc(wrote, 16)
            sp.wait_ge(wrote, 16)

        @b.tensor
        def _(pe):
            pe.wait_ge(loaded, 16 * loads)
            if bias is not None:
                m = nc.tensor.matmul(pb[:, 0:C], k.ones[0:1, 0:P], br[:, :], start=True, stop=not shared)
            if shared:
                pe.wait_ge(s_u, 1)
                m = nc.tensor.matmul(pb[:, 0:C], ub[:, :], wu[:, :], start=False, stop=True)
            if bias is not None:
                m.then_inc(s_b, 1)
            for t in range(T):
                for i in range(n):
                    q = t * n + i
                    if q >= 2:
                        pe.wait_ge(s_c, q - 1)
                    nc.tensor.transpose(pt[q % 2][:, 0:P], xs[i][:, t, :], k.ident[:, :]).then_inc(s_t, 1)
                    pe.wait_ge(s_c, q + 1)
                    if i == 0 and t >= 2:
                        pe.wait_ge(s_o, t - 1)
                    m = nc.tensor.matmul(ph[t % 2][:, 0:C], xt[:, q % 2, :], ws[i][:, :], start=i == 0, stop=i == n - 1)
                m.then_inc(s_h, 1)

        @b.scalar
        def _(a):
            for q in range(T * n):
                a.wait_ge(s_t, q + 1)
                if q >= 2 and q % n == 0:
                    a.wait_ge(s_h, (q - 2) // n + 1)
                nc.scalar.activation(xt[:, q % 2, :], pt[q % 2][:, 0:P], ACT.Copy).then_inc(s_c, 1)

        @b.vector
        def _(v):
            v.wait_ge(loaded, 16 * loads)
            if shared:
                v.tensor_scalar(ub[:, :], k.ones[:, :], ucol[:, 0:1], None, ALU.mult).then_inc(s_u, 1)
            if bias is None:
                v.memset(bb[:, :], 0.0).then_inc(s_bb, 1)
            else:
                v.wait_ge(s_b, 1)
                v.tensor_copy(bb[:, :], pb[:, 0:C]).then_inc(s_bb, 1)
            v.wait_ge(s_bb, 1)
            for t in range(T):
                v.wait_ge(s_h, t + 1)
                m = v.tensor_tensor(xs[0][:, t, :], ph[t % 2][:, 0:C], bb[:, :], ALU.add)
                if relu:
                    v.drain()
                    m = v.tensor_scalar(xs[0][:, t, :], xs[0][:, t, :], 0.0, None, ALU.max)
                if residual is not None:
                    v.drain()
                    m = v.tensor_tensor(xs[0][:, t, :], xs[0][:, t, :], res[:, t, :], ALU.add)
                m.then_inc(s_o, 1)


def aggregate(k, tag, xin, w, bias, tb, out, deg=None, w_own=None, relu=False):
    nc = k.nc
    with Phase(nc, tag) as f:
        x, parts = f.sb("x", [P, T, C], F32), f.sb("parts", [P, T, 3, C], BF16)
        wsb = f.sb("w", [C, C], F32)
        wo = f.sb("wo", [C, C], F32) if w_own is not None else None
        br, bb, xt = f.sb("br", [1, C], F32), f.sb("bb", [P, C], F32), f.sb("xt", [P, C], F32)
        blk = f.sb("blk", [P, 2, T, P], BF16)
        hs = f.sb("hs", [P, C], F32)
        scale, own = f.sb("scale", [P, T], F32), f.sb("own", [P, T], F32)
        pt, ph, pb = f.ps("pt", [P, PB]), f.ps("ph", [P, PB]), f.ps("pb", [P, PB])
        po = [f.ps(f"po{i}", [P, PB]) for i in range(2)]
        loaded, s_b, s_bb, s_t, s_c, s_h, s_p, s_dd, s_dr, wrote = [f.sem(x) for x in ("in", "b", "bb", "t", "c", "h", "p", "dd", "dr", "wr")]
        s_blk, s_use, s_o = [f.sem("blk0"), f.sem("blk1")], f.sem("use"), f.sem("o")
        loads = 3 + (w_own is not None)
        b = f.block()

        @b.sync
        def _(sp):
            sp.dma_start(x[:, :, :], nodes(xin)).then_inc(loaded, 16)
            sp.dma_start(wsb[:, :], w).then_inc(loaded, 16)
            sp.dma_start(br[:, :], bias.rearrange("(a n) -> a n", a=1)).then_inc(loaded, 16)
            if w_own is not None:
                sp.dma_start(wo[:, :], w_own).then_inc(loaded, 16)
            for t in range(T):
                if t >= 2:
                    sp.wait_ge(s_use, t - 1)
                sp.dma_start(blk[:, t % 2, :, :], tb[t]).then_inc(s_blk[t % 2], 16)
            sp.wait_ge(s_o, T)
            sp.dma_start(nodes(out), x[:, :, :]).then_inc(wrote, 16)
            sp.wait_ge(wrote, 16)

        @b.tensor
        def _(pe):
            pe.wait_ge(loaded, 16 * loads)
            nc.tensor.matmul(pb[:, 0:C], k.ones[0:1, 0:P], br[:, :], start=True, stop=True).then_inc(s_b, 1)
            for t in range(T):
                nc.tensor.transpose(pt[:, 0:P], x[:, t, :], k.ident[:, :]).then_inc(s_t, 1)
                pe.wait_ge(s_c, t + 1)
                if t:
                    pe.wait_ge(s_p, t)
                m = nc.tensor.matmul(ph[:, 0:C], xt[:, :], wsb[:, :], start=True, stop=True)
                if w_own is not None:
                    m = nc.tensor.matmul(ph[:, C:2 * C], xt[:, :], wo[:, :], start=True, stop=True)
                m.then_inc(s_h, 1)
            pe.wait_ge(s_p, T)
            for t in range(T):
                pe.wait_ge(s_blk[t % 2], 16 * (t // 2 + 1))
                if t >= 2:
                    pe.wait_ge(s_o, t - 1)
                for j in range(T):
                    m = nc.tensor.matmul(po[t % 2][:, 0:3 * C], blk[:, t % 2, j, :], parts[:, j, :, :].rearrange("p a c -> p (a c)"),
                                         start=j == 0, stop=j == T - 1)
                m.then_inc(s_use, 1)

        @b.scalar
        def _(a):
            if deg is not None:
                nc.scalar.activation(own[:, :], deg[:, :], ACT.Sqrt, bias=k.ones[:, 0:1]).then_inc(s_dd, 1)
            for t in range(T):
                a.wait_ge(s_t, t + 1)
                if t:
                    a.wait_ge(s_h, t)
                nc.scalar.activation(xt[:, :], pt[:, 0:P], ACT.Copy).then_inc(s_c, 1)

        @b.vector
        def _(v):
            if deg is not None:
                v.wait_ge(s_dd, 1)
                v.reciprocal(scale[:, :], own[:, :])
                v.drain()
                v.tensor_tensor(own[:, :], scale[:, :], scale[:, :], ALU.mult)
            else:
                v.tensor_scalar(own[:, :], k.count[:, :], 1.0, None, ALU.max)
                v.drain()
                v.reciprocal(scale[:, :], own[:, :])
            v.drain()
            v.wait_ge(s_b, 1)
            v.tensor_copy(bb[:, :], pb[:, 0:C]).then_inc(s_bb, 1)
            for t in range(T):
                v.wait_ge(s_h, t + 1)
                if deg is not None:
                    v.tensor_copy(x[:, t, :], ph[:, 0:C])
                    v.tensor_scalar(hs[:, :], ph[:, 0:C], scale[:, t:t + 1], None, ALU.mult)
                else:
                    v.tensor_copy(x[:, t, :], ph[:, C:2 * C])
                    v.tensor_copy(hs[:, :], ph[:, 0:C])
                v.drain()
                v.tensor_copy(parts[:, t, 0, :], hs[:, :])
                v.drain()
                v.tensor_tensor(hs[:, :], hs[:, :], parts[:, t, 0, :], ALU.subtract)
                v.drain()
                v.tensor_copy(parts[:, t, 1, :], hs[:, :])
                v.drain()
                v.tensor_tensor(parts[:, t, 2, :], hs[:, :], parts[:, t, 1, :], ALU.subtract).then_inc(s_p, 1)
            v.drain()
            for t in range(T):
                q = po[t % 2]
                v.wait_ge(s_use, t + 1)
                v.tensor_copy(hs[:, :], q[:, 2 * C:3 * C])
                v.drain()
                v.tensor_tensor(hs[:, :], hs[:, :], q[:, C:2 * C], ALU.add)
                v.drain()
                v.tensor_tensor(hs[:, :], hs[:, :], q[:, 0:C], ALU.add)
                v.drain()
                v.scalar_tensor_tensor(hs[:, :], hs[:, :], scale[:, t:t + 1], bb[:, :], ALU.mult, ALU.add)
                v.drain()
                if deg is not None:
                    m = v.scalar_tensor_tensor(x[:, t, :], x[:, t, :], own[:, t:t + 1], hs[:, :], ALU.mult, ALU.add)
                else:
                    m = v.tensor_tensor(x[:, t, :], x[:, t, :], hs[:, :], ALU.add)
                if relu:
                    v.drain()
                    m = v.tensor_scalar(x[:, t, :], x[:, t, :], 0.0, None, ALU.max)
                m.then_inc(s_o, 1)
                v.drain()


def to_rows(k, tag, col, row):
    nc = k.nc
    with Phase(nc, tag) as f:
        flat = f.sb("flat", [T, P], F32)
        pt = f.ps("pt", [P, PB])
        s_t, s_c, wrote = f.sem("t"), f.sem("c"), f.sem("wr")
        b = f.block()

        @b.tensor
        def _(pe):
            nc.tensor.transpose(pt[0:T, 0:P], col[:, :], k.ident[:, :]).then_inc(s_t, 1)

        @b.vector
        def _(v):
            v.wait_ge(s_t, 1)
            v.tensor_copy(flat[:, :], pt[0:T, 0:P]).then_inc(s_c, 1)

        @b.sync
        def _(sp):
            sp.wait_ge(s_c, 1)
            sp.dma_start(row.rearrange("a (t p) -> (a t) p", p=P), flat[:, :]).then_inc(wrote, 16)
            sp.wait_ge(wrote, 16)


def source_logits(k, l):
    nc = k.nc
    wp = [k.ins["L0_gnn_w_pool0"], k.ins["L0_gnn_w_pool1"], k.ins["L0_gnn_w_pool2"]][l]
    with Phase(nc, f"logit{l}") as f:
        x, wr, wb = f.sb("x", [P, T, C], F32), f.sb("wr", [1, C], F32), f.sb("wb", [P, C], F32)
        pw = f.ps("pw", [P, PB])
        loaded, s_w = f.sem("in"), f.sem("w")
        b = f.block()

        @b.sync
        def _(sp):
            sp.dma_start(x[:, :, :], nodes(k.X[l])).then_inc(loaded, 16)
            sp.dma_start(wr[:, :], wp[0:C, :].rearrange("c a -> a c")).then_inc(loaded, 16)

        @b.tensor
        def _(pe):
            pe.wait_ge(loaded, 32)
            nc.tensor.matmul(pw[:, 0:C], k.ones[0:1, 0:P], wr[:, :], start=True, stop=True).then_inc(s_w, 1)

        @b.vector
        def _(v):
            v.wait_ge(s_w, 1)
            v.wait_ge(loaded, 32)
            v.tensor_copy(wb[:, :], pw[:, 0:C])
            v.drain()
            v.tensor_tensor(x[:, :, :], x[:, :, :], wb[:, :].unsqueeze(1).to_broadcast([P, T, C]), ALU.mult)
            v.drain()
            v.tensor_reduce(k.ka[:, :], x[:, :, :], AX.X, ALU.add)
            v.drain()
            v.tensor_tensor(k.ka[:, :], k.ka[:, :], k.small[:, S_PAD:S_PAD + T], ALU.add)
    to_rows(k, f"logrow{l}", k.ka, k.rows[0:1, :])


def softmax_sums(k, l):
    nc = k.nc
    with Phase(nc, f"soft{l}") as f:
        ab, row = f.sb("ab", [P, NP], F32), f.sb("row", [P, NP], BF16)
        buf = [f.sb(f"buf{i}", [P, NP], F32) for i in range(2)]
        loaded, s_row, s_z, s_e, s_den, s_ln, s_s = [f.sem(x) for x in ("in", "row", "z", "e", "den", "ln", "s")]
        b = f.block()

        @b.sync
        def _(sp):
            sp.dma_start(ab[:, :], k.rows[0:1, :].to_broadcast([P, NP])).then_inc(loaded, 16)
            for t in range(T):
                if t:
                    sp.wait_ge(s_den, t)
                sp.dma_start(row[:, :], k.Drow[l][t * P:(t + 1) * P, :]).then_inc(s_row, 16)

        @b.vector
        def _(v):
            v.wait_ge(loaded, 16)

            def denominators(t):
                v.wait_ge(s_e, t + 1)
                v.wait_ge(s_row, 16 * (t + 1))
                v.tensor_tensor_reduce(out=buf[t % 2][:, :], in0=buf[t % 2][:, :], in1=row[:, :], scale=1.0, scalar=0.0,
                                       op0=ALU.mult, op1=ALU.add, accum_out=k.den[:, t:t + 1]).then_inc(s_den, 1)
            for t in range(T):
                if t >= 2:
                    v.drain()
                v.tensor_scalar(buf[t % 2][:, :], k.D[:, t, :], 0.5, NEG, ALU.is_lt, ALU.mult)
                v.drain()
                v.tensor_tensor_reduce(out=buf[t % 2][:, :], in0=buf[t % 2][:, :], in1=ab[:, :], scale=1.0, scalar=FAR,
                                       op0=ALU.add, op1=ALU.max, accum_out=k.top[:, t:t + 1])
                v.drain()
                v.tensor_scalar(buf[t % 2][:, :], ab[:, :], k.top[:, t:t + 1], 0.0, ALU.subtract, ALU.min).then_inc(s_z, 1)
                if t:
                    denominators(t - 1)
            denominators(T - 1)
            v.drain()
            v.tensor_scalar(k.den[:, :], k.den[:, :], 1e-18, None, ALU.max).then_inc(s_s, 1)
            v.wait_ge(s_ln, 1)
            v.tensor_tensor(k.kl[:, :], k.kl[:, :], k.top[:, :], ALU.add)
            v.drain()
            v.tensor_scalar(k.kl[:, :], k.kl[:, :], -1.0, None, ALU.mult)
            v.drain()
            v.tensor_tensor(k.kl[:, :], k.kl[:, :], k.small[:, S_PAD:S_PAD + T], ALU.add)

        @b.scalar
        def _(a):
            for t in range(T):
                a.wait_ge(s_z, t + 1)
                nc.scalar.activation(buf[t % 2][:, :], buf[t % 2][:, :], ACT.Exp).then_inc(s_e, 1)
            a.wait_ge(s_s, 1)
            nc.scalar.activation(k.kl[:, :], k.den[:, :], ACT.Ln).then_inc(s_ln, 1)
    to_rows(k, f"softrow{l}", k.kl, k.rows[1:2, :])


def ranks(k, tag, key, row, weights, table, own):
    nc = k.nc
    with Phase(nc, tag) as f:
        kb, iota = f.sb("kb", [P, NP], F32), f.sb("iota", [P, NP], I16)
        less, junk = f.sb("less", [P, 2, P], BF16), f.sb("junk", [P, NP], BF16)
        parts = f.sb("parts", [P, 4, T], F32)
        ra, rb = f.sb("ra", [P, T], F32), f.sb("rb", [P, T], F32)
        hi, lo, ei = f.sb("hi", [P, T], F32), f.sb("lo", [P, T], F32), f.sb("ei", [P, T], I32)
        ohk, cmp = f.sb("ohk", [P, T, K], F32), f.sb("cmp", [P, T, K], F32)
        ohl, val = f.sb("ohl", [P, 2, P], F32), f.sb("val", [P, 2, 2, K], F32)
        full = f.sb("full", [P, 2 * K], F32)
        pt = f.ps("pt", [P, PB])
        loaded, s_oh, s_mm = f.sem("in"), f.sem("oh"), f.sem("mm")
        b = f.block()

        @b.sync
        def _(sp):
            sp.dma_start(kb[:, :], row.to_broadcast([P, NP])).then_inc(loaded, 16)
            sp.dma_start(iota[:, :], k.ins["c_iota"]).then_inc(loaded, 16)

        @b.vector
        def _(v):
            def small(at):
                return k.small[:, at:at + K].unsqueeze(1).to_broadcast([P, T, K])

            def wide(col):
                return col[:, :].unsqueeze(2).to_broadcast([P, T, K])
            v.wait_ge(loaded, 32)
            v.memset(parts[:, :, :], 0.0)
            v.drain()
            for t in range(T):
                own_key, lo_c, hi_c = key[:, t:t + 1], t * P, (t + 1) * P
                v.tensor_scalar(less[:, t % 2, :], iota[:, lo_c:hi_c], k.small[:, S_ID + t:S_ID + t + 1], None, ALU.is_lt)
                v.tensor_scalar(junk[:, lo_c:hi_c], kb[:, lo_c:hi_c], own_key, 0.0, ALU.is_gt, ALU.add, accum_out=parts[:, 0, t:t + 1])
                if t:
                    v.tensor_scalar(junk[:, 0:lo_c], kb[:, 0:lo_c], own_key, 0.0, ALU.is_ge, ALU.add, accum_out=parts[:, 1, t:t + 1])
                if t < T - 1:
                    v.tensor_scalar(junk[:, hi_c:NP], kb[:, hi_c:NP], own_key, 0.0, ALU.is_gt, ALU.add, accum_out=parts[:, 2, t:t + 1])
                v.drain()
                v.scalar_tensor_tensor(junk[:, lo_c:hi_c], kb[:, lo_c:hi_c], own_key, less[:, t % 2, :], ALU.is_equal, ALU.mult, accum_out=parts[:, 3, t:t + 1])
                v.drain()
            v.tensor_reduce(ra[:, :], parts[:, :, :].rearrange("p i t -> p t i"), AX.X, ALU.add)
            v.drain()
            v.tensor_tensor(cmp[:, :, :], wide(ra), small(S_GJ), ALU.is_ge)
            v.drain()
            v.tensor_reduce(hi[:, :], cmp[:, :, :], AX.X, ALU.add)
            v.drain()
            v.tensor_scalar(lo[:, :], hi[:, :], -float(G), None, ALU.mult)
            v.drain()
            v.tensor_tensor(lo[:, :], lo[:, :], ra[:, :], ALU.add)
            v.tensor_tensor(ohk[:, :, :], wide(hi), small(S_T), ALU.is_equal)
            v.drain()
            v.tensor_scalar(rb[:, :], lo[:, :], -2.0, float(EXP0), ALU.mult, ALU.add)
            v.drain()
            v.tensor_copy(ei[:, :], rb[:, :])
            v.tensor_scalar(own[:, :], hi[:, :], -256.0, 256.0 * (K - 1), ALU.mult, ALU.add)
            v.drain()
            v.tensor_tensor(own[:, :], own[:, :], rb[:, :], ALU.add)
            v.tensor_scalar(ei[:, :], ei[:, :], 23, None, ALU.logical_shift_left)
            v.drain()
            v.tensor_tensor(weights[:, :, :], ohk[:, :, :], wide(ei[:, :].bitcast(F32)), ALU.mult)
            for t in range(T):
                if t >= 2:
                    v.wait_ge(s_mm, t - 1)
                v.tensor_scalar(ohl[:, t % 2, :], iota[:, 0:P], lo[:, t:t + 1], None, ALU.is_equal)
                v.tensor_scalar(val[:, t % 2, 0, :], ohk[:, t, :], key[:, t:t + 1], None, ALU.mult)
                v.tensor_scalar(val[:, t % 2, 1, :], ohk[:, t, :], k.small[:, S_ID + t:S_ID + t + 1], None, ALU.mult).then_inc(s_oh, 1)
                v.drain()
            v.wait_ge(s_mm, T)
            v.tensor_copy(full[:, :], pt[:, 0:2 * K])
            v.drain()
            for i in range(3):
                v.tensor_copy(table[:, i, :], full[:, :])
                v.drain()
                v.tensor_tensor(full[:, :], full[:, :], table[:, i, :], ALU.subtract)
                v.drain()

        @b.tensor
        def _(pe):
            for t in range(T):
                pe.wait_ge(s_oh, t + 1)
                nc.tensor.matmul(pt[:, 0:2 * K], ohl[:, t % 2, :], val[:, t % 2, :, :].rearrange("p a k -> p (a k)"),
                                 start=t == 0, stop=t == T - 1).then_inc(s_mm, 1)


def match(k, l, wa, wl, ta, tl, ownl, sizes):
    nc = k.nc
    with Phase(nc, f"match{l}") as f:
        sb = f.sb
        left = sb("left", [P, T], F32)
        va, vl = sb("va", [P, T, K], BF16), sb("vl", [P, T, K], BF16)
        eis, eos = sb("ei", [P, 2 * T * K], I32), sb("eo", [P, 2 * T * K], F32)
        masks = sb("mask", [P, 2 * T * K], F32)
        keys, codes = sb("key", [P, 2 * T], F32), sb("code", [P, 2 * T], F32)
        ints, parts_i = sb("ints", [P, 2 * T], I32), sb("partsi", [P, 2 * T], I32)
        rowt, sel = sb("rowt", [T, 2 * P], BF16), sb("sel", [T, NP], BF16)
        ohs = [sb(f"oh{i}", [P, NP], BF16) for i in range(2)]
        prod = eis[:, :].bitcast(F32)
        got = sb("got", [P, 2 * T * 2], F32)
        back = sb("back", [P, T], F32)
        kk = sb("kk", [P, 2, T], F32)
        e, some = sb("e", [P, 2 * T], F32), sb("some", [P, 2 * T], F32)
        isin, tie, any_, mate, hit = [sb(x, [P, T], F32) for x in ("isin", "tie", "any", "mate", "hit")]
        matet = sb("matet", [P, 2, K], BF16)
        mates, ins, t1, t2 = [sb(x, [P, T], F32) for x in ("mates", "ins", "t1", "t2")]
        hits, flag = sb("hits", [P, 1], F32), sb("flag", [P, 1], I32)
        ps = f.ps("ps", [P, 8 * PB])
        TR = 7 * PB
        s_sel, s_v, s_best, s_e, s_tr, s_tc, s_bc, s_oh, s_g, s_gs, s_mt, s_cnt, s_tot, s_flag, s_seen, s_ti = [
            f.sem(x) for x in ("sel", "v", "best", "e", "tr", "tc", "bc", "oh", "g", "gs", "mt", "cnt", "tot", "flag", "seen", "ti")]
        b = f.block()

        def small(n):
            return n <= 16

        def fetch_bank(n, q):
            return 4 * PB if small(n) and q != 1 else 0

        @b.sync
        def _(sp):
            sp.dma_start(eos[0:T, 0:NP // 4], k.ins["c_sel"][:, 0:NP // 4]).then_inc(s_sel, 16)
            for i in range(1, 4):
                sp.wait_ge(s_ti, i)
                sp.dma_start(eos[0:T, 0:NP // 4], k.ins["c_sel"][:, i * NP // 4:(i + 1) * NP // 4]).then_inc(s_sel, 16)

        @b.vector
        def _(v):
            def tt(out, a, c, op):
                v.tensor_tensor(out, a, c, op)
                v.drain()

            def ts(out, a, s1, s2, op0, op1=ALU.bypass):
                v.tensor_scalar(out, a, s1, s2, op0, op1)
                v.drain()

            def wide(col):
                return col.unsqueeze(2).to_broadcast([P, col.shape[1], K])

            for i in range(4):
                v.wait_ge(s_sel, 16 * (i + 1))
                v.tensor_copy(sel[:, i * NP // 4:(i + 1) * NP // 4], eos[0:T, 0:NP // 4]).then_inc(s_ti, 1)
            v.memset(left[:, :], 1.0)
            v.memset(mates[:, :], 0.0)
            v.memset(ins[:, :], 0.0)
            v.memset(matet[:, :, :], -1.0)
            v.tensor_copy(kk[:, 0, :], k.kl[:, :])
            v.tensor_copy(kk[:, 1, :], k.ka[:, :])
            v.tensor_copy(va[:, :, :], wa[:, :, :]).then_inc(s_v, 1)
            v.tensor_copy(vl[:, :, :], wl[:, :, :]).then_inc(s_v, 1)
            v.drain()
            done = v.alloc_register(f"done{l}")
            more = v.alloc_register(f"more{l}")
            v.reg_mov(done, 0)

            def one_hot(n, r, q, scal):
                v.wait_ge(s_bc, r * 3 + q + 1)
                v.tensor_scalar(ohs[q % 2][:, 0:n * P], ps[:, 0:n * P], scal, None, ALU.is_equal).then_inc(s_oh, 1)

            def take(n, r, q, mask, a, out):
                v.wait_ge(s_g, r * 3 + q + 1)
                per = PB // (a * K) // 5 * 5
                pr = prod[:, 0:n * a * K].rearrange("p (t a k) -> p t a k", a=a, k=K)
                for j in range(0, n, per):
                    w = min(per, n - j)
                    at = fetch_bank(n, q) + j // per * PB
                    m = v.tensor_tensor(pr[:, j:j + w, :, :], ps[:, at:at + w * a * K].rearrange("p (t a k) -> p t a k", a=a, k=K),
                                        mask[:, j:j + w, :].unsqueeze(2).to_broadcast([P, w, a, K]), ALU.mult)
                m.then_inc(s_gs, 1)
                v.drain()
                v.tensor_reduce(out, prod[:, 0:n * a * K].rearrange("p (x k) -> p x k", k=K), AX.X, ALU.add)
                v.drain()

            def round_of(n):
                left_, isin_, tie_, any_n, mate_, hit_, mates_, ins_, t1_, t2_, own_, idc, back_ = [
                    x[:, 0:n] for x in (left, isin, tie, any_, mate, hit, mates, ins, t1, t2, ownl, k.small[:, S_ID:S_ID + T], back)]
                r = v.snap(done)
                key, code, e_, some_ = [x[:, 0:2 * n] for x in (keys, codes, e, some)]
                int_, part_ = ints[:, 0:2 * n], parts_i[:, 0:2 * n]
                for d0, d1 in ([(0, 2)] if small(n) else [(0, 1), (1, 2)]):
                    v.wait_ge(s_best, r * 2 + d1)
                    ei = eis[:, 0:2 * n * K].rearrange("p (d t k) -> p d t k", d=2, k=K)
                    sums = ps[:, 0:4 * PB].bitcast(I32).rearrange("p (d n) -> p d n", d=2)
                    for j in range(0, n, 20):
                        w = min(20, n - j)
                        part = sums[:, d0:d1, j // 20 * PB:j // 20 * PB + w * K].rearrange("p d (t k) -> p d t k", k=K)
                        v.tensor_scalar(ei[:, d0:d1, j:j + w, :], part, 23, None, ALU.logical_shift_right)
                    v.drain()
                    e3 = eis[:, d0 * n * K:d1 * n * K].rearrange("p (x k) -> p x k", k=K)
                    o3 = eos[:, d0 * n * K:d1 * n * K].rearrange("p (x k) -> p x k", k=K)
                    v.scalar_tensor_tensor(o3, e3, 0.0, k.small[:, S_OFF:S_OFF + K].unsqueeze(1).to_broadcast([P, (d1 - d0) * n, K]), ALU.is_gt, ALU.mult)
                    v.drain()
                    tt(o3, o3, e3, ALU.add)
                    v.tensor_reduce(keys[:, d0 * n:d1 * n], o3, AX.X, ALU.max)
                    v.drain()
                v.tensor_copy(int_, key)
                v.drain()
                ts(part_, int_, 255, None, ALU.bitwise_and)
                v.tensor_copy(code, part_)
                v.drain()
                v.sem_inc(s_e, 1)
                o3 = eos[:, 0:2 * n * K].rearrange("p (x k) -> p x k", k=K)
                m3 = masks[:, 0:2 * n * K].rearrange("p (x k) -> p x k", k=K)
                tt(m3, o3, wide(key), ALU.is_equal)
                v.wait_ge(s_tr, r * 2 + 1)
                v.tensor_copy(rowt[0:n, :], ps[0:n, TR:TR + 2 * P]).then_inc(s_tc, 1)
                ts(some_, key, 0.5, None, ALU.is_gt)
                tt(any_n, some_[:, 0:n], some_[:, n:2 * n], ALU.max)
                tt(any_n, any_n, left_, ALU.mult)
                ts(some_, some_, SHUT, -SHUT, ALU.mult, ALU.add)
                tt(tie_, own_, key[:, n:2 * n], ALU.is_ge)
                cq = k.small[:, S_CQ:S_CQ + 1]
                one_hot(n, r, 0, cq)
                if small(n):
                    one_hot(n, r, 1, cq)
                take(n, r, 0, m3[:, 0:n, :], 2, got[:, 0:2 * n])
                if not small(n):
                    one_hot(n, r, 1, cq)
                take(n, r, 1, m3[:, n:2 * n, :], 2, got[:, 2 * n:4 * n])
                g = got[:, 0:4 * n].rearrange("p (d t a) -> p d t a", d=2, a=2)
                e2 = e_.rearrange("p (d t) -> p d t", d=2)
                tt(e2, g[:, :, :, 0], kk[:, :, 0:n], ALU.add)
                tt(e_, e_, some_, ALU.add)
                tt(t1_, e_[:, 0:n], e_[:, n:2 * n], ALU.is_equal)
                v.tensor_tensor(isin_, e_[:, 0:n], e_[:, n:2 * n], ALU.is_gt)
                tt(tie_, tie_, t1_, ALU.mult)
                tt(isin_, isin_, tie_, ALU.add)
                tt(t1_, g[:, 0, :, 1], g[:, 1, :, 1], ALU.subtract)
                tt(t1_, t1_, isin_, ALU.mult)
                tt(t1_, t1_, g[:, 1, :, 1], ALU.add)
                v.scalar_tensor_tensor(mate_, t1_, 1.0, any_n, ALU.add, ALU.mult)
                v.drain()
                ts(int_[:, 0:n], mate_, -1.0, None, ALU.add)
                v.tensor_scalar(part_[:, 0:n], int_[:, 0:n], P - 1, None, ALU.bitwise_and)
                ts(part_[:, n:2 * n], int_[:, 0:n], 7, None, ALU.arith_shift_right)
                v.tensor_copy(code, part_)
                v.drain()
                v.sem_inc(s_e, 1)
                v.tensor_scalar(matet[:, 0, 0:n], code[:, n:2 * n], float(P), None, ALU.mult)
                v.tensor_copy(matet[:, 1, 0:n], code[:, 0:n]).then_inc(s_mt, 1)
                tt(m3[:, 0:n, :], wide(code[:, n:2 * n]), k.small[:, S_T:S_T + K].unsqueeze(1).to_broadcast([P, n, K]), ALU.is_equal)
                v.wait_ge(s_tr, r * 2 + 2)
                v.tensor_copy(rowt[0:n, 0:P], ps[0:n, TR:TR + P]).then_inc(s_tc, 1)
                one_hot(n, r, 2, k.small[:, S_P:S_P + 1])
                take(n, r, 2, m3[:, 0:n, :], 1, back_)
                tt(hit_, back_, idc, ALU.is_equal)
                tt(hit_, hit_, any_n, ALU.mult)
                tt(left_, left_, hit_, ALU.subtract)
                v.tensor_tensor(va[:, 0:n, :], wa[:, 0:n, :], wide(left_), ALU.mult).then_inc(s_v, 1)
                v.tensor_reduce(hits[:, :], hit_, AX.X, ALU.add).then_inc(s_cnt, 1)
                v.tensor_tensor(vl[:, 0:n, :], wl[:, 0:n, :], wide(left_), ALU.mult).then_inc(s_v, 1)
                v.tensor_tensor(t1_, mate_, hit_, ALU.mult)
                tt(t2_, isin_, hit_, ALU.mult)
                v.tensor_tensor(mates_, mates_, t1_, ALU.add)
                v.tensor_tensor(ins_, ins_, t2_, ALU.add)
                v.reg_add(done, done, 1)
                now = v.snap(done)
                v.wait_ge(s_tot, now)
                v.tensor_copy(flag[:, :], ps[:, TR:TR + 1]).then_inc(s_flag, 1)
                v.wait_ge(s_flag, now)
                v.sem_inc(s_seen, 1)
                v.load(more, flag[0:1, 0:1])

            for which, n in enumerate(sizes):
                v.load(more, k.runs[0:1, which:which + 1])
                with v.While(nc.lower_val(more)):
                    round_of(n)
            v.drain()
            idc = k.small[:, S_ID:S_ID + T]
            ts(mate[:, :], mates[:, :], -1.0, None, ALU.add)
            ts(hit[:, :], left[:, :], -1.0, 1.0, ALU.mult, ALU.add)
            tt(tie[:, :], mate[:, :], idc, ALU.is_equal)
            tt(tie[:, :], tie[:, :], hit[:, :], ALU.mult)
            tt(t2[:, :], hit[:, :], ins[:, :], ALU.subtract)
            tt(t1[:, :], ins[:, :], tie[:, :], ALU.subtract)
            tt(isin[:, :], mate[:, :], idc, ALU.subtract)
            tt(isin[:, :], isin[:, :], t1[:, :], ALU.mult)
            tt(k.cl[l][:, :], isin[:, :], idc, ALU.add)
            v.scalar_tensor_tensor(isin[:, :], mate[:, :], -float(ZERO), t2[:, :], ALU.add, ALU.mult)
            v.drain()
            ts(k.m2[:, :], isin[:, :], float(ZERO), None, ALU.add)
            tt(tie[:, :], tie[:, :], t2[:, :], ALU.add)
            v.scalar_tensor_tensor(isin[:, :], mate[:, :], -float(ZERO), tie[:, :], ALU.add, ALU.mult)
            v.drain()
            ts(k.om[:, :], isin[:, :], float(ZERO), None, ALU.add)

        @b.tensor
        def _(pe):
            pe.wait_ge(s_ti, 4)
            done = pe.alloc_register(f"done{l}")
            more = pe.alloc_register(f"more{l}")
            pe.reg_mov(done, 0)

            def best(n, mat, w, at):
                for t in range(n):
                    o = at + (t // 20) * PB + (t % 20) * K
                    for j in range(n):
                        m = nc.tensor.matmul(ps[:, o:o + K], mat[:, j, t * P:(t + 1) * P], w[:, j, :], start=j == 0, stop=j == n - 1)
                m.then_inc(s_best, 1)

            def spread(n, row):
                for t in range(n):
                    m = nc.tensor.matmul(ps[:, t * P:(t + 1) * P], sel[0:n, t * P:(t + 1) * P], rowt[0:n, row:row + P], start=True, stop=True)
                m.then_inc(s_bc, 1)

            def fetch(n, r, q, tables, a):
                pe.wait_ge(s_oh, r * 3 + q + 1)
                per = PB // (a * K) // 5 * 5
                for t in range(n):
                    o = fetch_bank(n, q) + t // per * PB + t % per * a * K
                    for i, tab in enumerate(tables):
                        m = nc.tensor.matmul(ps[:, o:o + a * K], ohs[q % 2][:, t * P:(t + 1) * P], tab, start=i == 0, stop=i == len(tables) - 1)
                m.then_inc(s_g, 1)

            def round_of(n):
                r = pe.snap(done)
                pe.wait_ge(s_v, r * 2 + 2)
                nc.tensor.matmul(ps[:, TR:TR + 1], k.identb[:, :], k.identb[:, 0:1], start=True, stop=True)
                best(n, k.Tm, va, 0)
                best(n, k.D, vl, 2 * PB)
                pe.wait_ge(s_e, r * 2 + 1)
                for d in range(2):
                    m = nc.tensor.transpose(ps[0:n, TR + d * P:TR + (d + 1) * P], codes[:, d * n:(d + 1) * n], k.ident[:, :])
                m.then_inc(s_tr, 1)
                pe.wait_ge(s_tc, r * 2 + 1)
                tas, tls = [ta[:, i, :] for i in range(3)], [tl[:, i, :] for i in range(3)]
                spread(n, 0)
                if small(n):
                    pe.wait_ge(s_oh, r * 3 + 1)
                    spread(n, P)
                    fetch(n, r, 0, tas, 2)
                else:
                    fetch(n, r, 0, tas, 2)
                    pe.wait_ge(s_gs, r * 3 + 1)
                    spread(n, P)
                fetch(n, r, 1, tls, 2)
                pe.wait_ge(s_e, r * 2 + 2)
                nc.tensor.transpose(ps[0:n, TR:TR + P], codes[:, 0:n], k.ident[:, :]).then_inc(s_tr, 1)
                pe.wait_ge(s_tc, r * 2 + 2)
                spread(n, 0)
                pe.wait_ge(s_mt, r + 1)
                fetch(n, r, 2, [matet[:, i, :] for i in range(2)], 1)
                pe.wait_ge(s_cnt, r + 1)
                nc.tensor.matmul(ps[:, TR:TR + 1], k.ones[:, 0:P], hits[:, :], start=True, stop=True).then_inc(s_tot, 1)
                pe.reg_add(done, done, 1)
                now = pe.snap(done)
                pe.wait_ge(s_flag, now)
                pe.sem_inc(s_seen, 1)
                pe.load(more, flag[0:1, 0:1])

            for which, n in enumerate(sizes):
                pe.load(more, k.runs[0:1, which:which + 1])
                with pe.While(nc.lower_val(more)):
                    round_of(n)


def gather_rows(pool, done, out, table, index):
    for t in range(T):
        pool.indirect_dma_start(out[:, t, :], None, table, bass.IndirectOffsetOnAxis(index[:, t:t + 1], 0)).then_inc(done, 16)


def compact(k, l, next_sizes):
    nc = k.nc
    with Phase(nc, f"comp{l}") as f:
        sb = f.sb
        rep, pos, t1, t2, lo, hi = [sb(x, [P, T], F32) for x in ("rep", "pos", "t1", "t2", "lo", "hi")]
        m2f, omf, tot, offs, score = [sb(x, [P, T], F32) for x in ("m2f", "omf", "tot", "offs", "score")]
        ii, jj = sb("ii", [P, T], I32), sb("jj", [P, T], I32)
        cmp, ohk = sb("cmp", [P, T, T], F32), sb("ohk", [P, T, K], F32)
        ohl, val = sb("ohl", [P, 2, P], F32), sb("val", [P, 2, 2, K], F32)
        tri, iota = sb("tri", [P, P], F32), sb("iota", [P, P], I16)
        tab, gc, go, last = sb("tab", [P, T, 4], F32), sb("gc", [P, T, 4], F32), sb("go", [P, T, 4], F32), sb("last", [1, 4], F32)
        fl = sb("fl", [P, 4], F32)
        pt, pp = f.ps("pt", [P, PB]), f.ps("pp", [P, PB])
        loaded, s_rep, s_pre, s_oh, s_mm, s_tab, s_w, s_g, s_m, s_x, s_e, s_sc, s_w2, s_g2 = [f.sem(x) for x in (
            "in", "rep", "pre", "oh", "mm", "tab", "w", "g", "m", "x", "e", "sc", "w2", "g2")]
        idc = k.small[:, S_ID:S_ID + T]
        st = k.small[:, S_T:S_T + T]
        tabd = k.tab[0:NP, :].rearrange("(t p) c -> p t c", p=P)
        b = f.block()

        @b.sync
        def _(sp):
            sp.dma_start(tri[:, :], k.ins["c_tri"]).then_inc(loaded, 16)
            sp.dma_start(iota[:, :], k.ins["c_iota"][:, 0:P]).then_inc(loaded, 16)
            sp.wait_ge(s_tab, 1)
            sp.dma_start(tabd, tab[:, :, :]).then_inc(s_w, 16)
            sp.dma_start(k.tab[ZERO:ZERO + 1, :], last[:, :]).then_inc(s_w, 16)
            sp.wait_ge(s_sc, 1)
            sp.dma_start(tabd, tab[:, :, :]).then_inc(s_w2, 16)

        @b.gpsimd
        def _(pool):
            pool.wait_ge(s_w, 32)
            gather_rows(pool, s_g, gc, k.tab[:, :], k.cl[l])
            gather_rows(pool, s_g, go, k.tab[:, :], k.om)
            pool.wait_ge(s_w2, 16)
            pool.wait_ge(s_m, 1)
            pool.wait_ge(s_x, 1)
            gather_rows(pool, s_g2, gc, k.tab[:, :], k.m1)

        @b.tensor
        def _(pe):
            pe.wait_ge(loaded, 32)
            pe.wait_ge(s_rep, 1)
            nc.tensor.matmul(pp[:, 0:T], tri[:, :], rep[:, :], start=True, stop=True)
            nc.tensor.matmul(pp[:, T:2 * T], k.ones[:, 0:P], rep[:, :], start=True, stop=True).then_inc(s_pre, 1)
            for t in range(T):
                pe.wait_ge(s_oh, t + 1)
                nc.tensor.matmul(pt[:, 0:2 * K], ohl[:, t % 2, :], val[:, t % 2, :, :].rearrange("p a k -> p (a k)"),
                                 start=t == 0, stop=t == T - 1).then_inc(s_mm, 1)

        @b.scalar
        def _(a):
            a.wait_ge(s_x, 1)
            nc.scalar.activation(score[:, :], t1[:, :], ACT.Exp).then_inc(s_e, 1)

        @b.vector
        def _(v):
            def tt(out, a, c, op):
                v.tensor_tensor(out, a, c, op)
                v.drain()

            def ts(out, a, s1, s2, op0, op1=ALU.bypass):
                v.tensor_scalar(out, a, s1, s2, op0, op1)
                v.drain()

            def copy(out, a):
                v.tensor_copy(out, a)
                v.drain()
            v.wait_ge(loaded, 32)
            v.memset(last[:, :], 1.0)
            v.memset(tab[:, :, :], 0.0)
            copy(t1[:, :], k.cl[l][:, :])
            copy(m2f[:, :], k.m2[:, :])
            copy(omf[:, :], k.om[:, :])
            tt(rep[:, :], t1[:, :], idc, ALU.is_equal)
            ts(t2[:, :], idc, k.n[l][:, 0:1], None, ALU.is_lt)
            tt(rep[:, :], rep[:, :], t2[:, :], ALU.mult)
            v.sem_inc(s_rep, 1)
            v.wait_ge(s_pre, 1)
            copy(tot[:, :], pp[:, T:2 * T])
            copy(pos[:, :], pp[:, 0:T])
            tt(cmp[:, :, :], st.unsqueeze(1).to_broadcast([P, T, T]), st.unsqueeze(2).to_broadcast([P, T, T]), ALU.is_lt)
            tt(cmp[:, :, :], cmp[:, :, :], tot[:, :].unsqueeze(1).to_broadcast([P, T, T]), ALU.mult)
            v.tensor_reduce(offs[:, :], cmp[:, :, :], AX.X, ALU.add)
            v.tensor_reduce(k.n[l + 1][:, :], tot[:, :], AX.X, ALU.add)
            v.drain()
            tt(pos[:, :], pos[:, :], offs[:, :], ALU.add)
            below = -1.0
            for i, s in enumerate(next_sizes):
                ts(fl[:, 0:1], k.n[l + 1][:, :], below, None, ALU.is_gt)
                ts(fl[:, 1:2], k.n[l + 1][:, :], float(s * P), None, ALU.is_le)
                tt(fl[:, 0:1], fl[:, 0:1], fl[:, 1:2], ALU.mult)
                copy(k.runs[:, i:i + 1], fl[:, 0:1])
                below = float(s * P)
            v.scalar_tensor_tensor(t1[:, :], pos[:, :], 1.0, rep[:, :], ALU.add, ALU.mult)
            v.drain()
            ts(t1[:, :], t1[:, :], -1.0, None, ALU.add)
            copy(ii[:, :], t1[:, :])
            ts(jj[:, :], ii[:, :], 127, None, ALU.bitwise_and)
            copy(lo[:, :], jj[:, :])
            ts(jj[:, :], ii[:, :], 7, None, ALU.arith_shift_right)
            copy(hi[:, :], jj[:, :])
            tt(ohk[:, :, :], hi[:, :].unsqueeze(2).to_broadcast([P, T, K]), k.small[:, S_T:S_T + K].unsqueeze(1).to_broadcast([P, T, K]), ALU.is_equal)
            ts(t1[:, :], idc, -float(ZERO), None, ALU.add)
            ts(t2[:, :], m2f[:, :], -float(ZERO), None, ALU.add)
            for t in range(T):
                if t >= 2:
                    v.wait_ge(s_mm, t - 1)
                v.tensor_scalar(ohl[:, t % 2, :], iota[:, :], lo[:, t:t + 1], None, ALU.is_equal)
                v.tensor_scalar(val[:, t % 2, 0, :], ohk[:, t, :], t1[:, t:t + 1], None, ALU.mult)
                v.tensor_scalar(val[:, t % 2, 1, :], ohk[:, t, :], t2[:, t:t + 1], None, ALU.mult).then_inc(s_oh, 1)
                v.drain()
            copy(tab[:, :, 0], pos[:, :])
            copy(tab[:, :, 1], k.top[:, :])
            copy(tab[:, :, 2], k.den[:, :])
            v.sem_inc(s_tab, 1)
            v.wait_ge(s_mm, T)
            ts(t2[:, :], pt[:, 0:K], float(ZERO), None, ALU.add)
            copy(k.m1[:, :], t2[:, :])
            ts(t2[:, :], pt[:, K:2 * K], float(ZERO), None, ALU.add)
            copy(k.m2[:, :], t2[:, :])
            v.sem_inc(s_m, 1)
            v.wait_ge(s_g, 32 * T)
            copy(k.cl[l][:, :], gc[:, :, 0])
            tt(t1[:, :], k.ka[:, :], go[:, :, 1], ALU.subtract)
            ts(t1[:, :], t1[:, :], 0.0, None, ALU.min)
            ts(omf[:, :], omf[:, :], float(ZERO), None, ALU.is_lt)
            ts(t2[:, :], go[:, :, 2], 1e-18, None, ALU.max)
            v.reciprocal(t2[:, :], t2[:, :])
            v.drain()
            v.sem_inc(s_x, 1)
            v.wait_ge(s_e, 1)
            tt(t2[:, :], t2[:, :], score[:, :], ALU.mult)
            v.scalar_tensor_tensor(t2[:, :], t2[:, :], -0.5, omf[:, :], ALU.add, ALU.mult)
            v.drain()
            ts(tab[:, :, 0], t2[:, :], 1.0, None, ALU.add)
            v.sem_inc(s_sc, 1)
            v.wait_ge(s_g2, 16 * T)
            v.tensor_copy(k.ss[l][:, :], gc[:, :, 0])


def pool_rows(k, l):
    nc = k.nc
    with Phase(nc, f"prow{l}") as f:
        x1, x2 = f.sb("x1", [P, T, C], F32), f.sb("x2", [P, T, C], F32)
        s_c, s_g, s_x, wrote = [f.sem(x) for x in ("c", "g", "x", "wr")]
        b = f.block()

        @b.sync
        def _(sp):
            sp.dma_start(k.Xg[0:NP, :], k.X[l][:, :]).then_inc(s_c, 16)
            sp.wait_ge(s_x, 1)
            sp.dma_start(nodes(k.Xc), x1[:, :, :]).then_inc(wrote, 16)
            sp.wait_ge(wrote, 16)

        @b.gpsimd
        def _(pool):
            pool.wait_ge(s_c, 16)
            gather_rows(pool, s_g, x1, k.Xg[:, :], k.m1)
            gather_rows(pool, s_g, x2, k.Xg[:, :], k.m2)

        @b.vector
        def _(v):
            v.wait_ge(s_g, 32 * T)
            v.tensor_tensor(x1[:, :, :], x1[:, :, :], x2[:, :, :], ALU.add)
            v.drain()
            v.tensor_tensor(x1[:, :, :], x1[:, :, :], k.ss[l][:, :].unsqueeze(2).to_broadcast([P, T, C]), ALU.mult).then_inc(s_x, 1)


def unpool_rows(k, l):
    nc = k.nc
    with Phase(nc, f"urow{l}") as f:
        x1, x2, inv = f.sb("x1", [P, T, C], F32), f.sb("x2", [P, T, C], F32), f.sb("inv", [P, T], F32)
        loaded, s_d, s_c, s_g, s_x, wrote = [f.sem(x) for x in ("in", "d", "c", "g", "x", "wr")]
        b = f.block()

        @b.sync
        def _(sp):
            sp.dma_start(x1[:, :, :], nodes(k.Xc)).then_inc(loaded, 16)
            sp.dma_start(x2[:, :, :], nodes(k.X[l])).then_inc(loaded, 16)
            sp.wait_ge(s_d, 1)
            sp.dma_start(nodes(k.Xg), x1[:, :, :]).then_inc(s_c, 16)
            sp.wait_ge(s_x, 1)
            sp.dma_start(nodes(k.Xc), x1[:, :, :]).then_inc(wrote, 16)
            sp.wait_ge(wrote, 16)

        @b.gpsimd
        def _(pool):
            pool.wait_ge(s_c, 16)
            gather_rows(pool, s_g, x1, k.Xg[:, :], k.cl[l])

        @b.vector
        def _(v):
            v.reciprocal(inv[:, :], k.ss[l][:, :])
            v.wait_ge(loaded, 32)
            v.drain()
            v.tensor_tensor(x1[:, :, :], x1[:, :, :], inv[:, :].unsqueeze(2).to_broadcast([P, T, C]), ALU.mult).then_inc(s_d, 1)
            v.wait_ge(s_g, 16 * T)
            v.tensor_tensor(x1[:, :, :], x1[:, :, :], x2[:, :, :], ALU.add).then_inc(s_x, 1)


def coarsen(k, l):
    nc = k.nc
    n = l + 1
    segs = k.RT[0:NP, :].rearrange("(j p) (i c) -> i p j c", p=P, c=P)

    def buf(q):
        return q % T % 2

    def count(q):
        return (q // T) * ((T + 1 - buf(q)) // 2) + q % T // 2 + 1
    with Phase(nc, f"coar{l}") as f:
        g = [[f.sb(f"g{m}{u}", [P, NP], BF16) for u in range(2)] for m in range(2)]
        blk, iota = [f.sb(f"blk{u}", [P, T, P], BF16) for u in range(2)], f.sb("iota", [P, NP], I16)
        pt = [f.ps(f"pt{u}", [P, 4 * PB]) for u in range(2)]
        ptb = [x[:, :].bitcast(BF16) for x in pt]
        s_i, s_g, s_rt, s_sum, s_tr, s_blk, s_own, s_w, s_deg = [
            f.sem("i"), [f.sem(f"g{u}") for u in range(2)], [f.sem(f"rt{u}") for u in range(2)],
            f.sem("sum"), f.sem("tr"), f.sem("blk"), f.sem("own"), [f.sem("w0"), f.sem("w1")], f.sem("deg")]
        both = n < DEPTH
        b = f.block()

        def stored(q):
            last = q if both else min(q, T - 1)
            return (last - q % 2) // 2 + 1

        @b.gpsimd
        def _(pool):
            for q in range(2 * T):
                i = q % T
                if q == T:
                    for u in range(2):
                        pool.wait_ge(s_w[u], 16 * ((T + 1 - u) // 2))
                if q >= 2:
                    pool.wait_ge(s_tr, q - 1)
                    if q >= T + 2:
                        pool.wait_ge(s_rt[i % 2], 16 * (i // 2))
                        pool.wait_ge(s_deg, q - T - 1)
                table = k.Drow[l] if q < T else k.RT
                for m, ix in enumerate((k.m1, k.m2)):
                    pool.indirect_dma_start(g[m][buf(q)][:, :], None, table[:, :],
                                            bass.IndirectOffsetOnAxis(ix[:, i:i + 1], 0)).then_inc(s_g[buf(q)], 16)

        @b.vector
        def _(v):
            v.wait_ge(s_i, 16)

            def keep(q):
                i = q - T
                v.wait_ge(s_blk, q + 1)
                v.tensor_copy(k.D[:, :, i * P:(i + 1) * P], blk[q % 2][:, :, :], saturate=False).then_inc(s_own, 1)
            for q in range(2 * T):
                i, a, c = q % T, g[0][buf(q)], g[1][buf(q)]
                v.wait_ge(s_g[buf(q)], 32 * count(q))
                m = v.tensor_tensor(a[:, :], a[:, :], c[:, :], ALU.add)
                if q >= T:
                    v.drain()
                    v.tensor_scalar(c[:, :], iota[:, :], k.small[:, S_ID + i:S_ID + i + 1], None, ALU.not_equal)
                    v.drain()
                    m = v.scalar_tensor_tensor(a[:, :], a[:, :], 1.0, c[:, :], ALU.min, ALU.mult)
                m.then_inc(s_sum, 1)
                if q > T:
                    v.drain()
                    keep(q - 1)
            keep(2 * T - 1)
            v.drain()
            for t in range(T):
                v.tensor_scalar(g[1][0][:, :], k.D[:, t, :], 1.0, 0.0, ALU.mult, ALU.add, accum_out=k.deg[n][:, t:t + 1])
                v.drain()

        @b.scalar
        def _(a):
            for q in range(2 * T):
                if q >= T:
                    a.wait_ge(s_sum, q + 1)
                    nc.scalar.activation(k.Tm[:, q - T, :], g[0][buf(q)][:, :], ACT.Copy, saturate=False).then_inc(s_deg, 1)
                a.wait_ge(s_tr, q + 1)
                if q >= 2:
                    a.wait_ge(s_w[q % 2], 16 * stored(q - 2))
                if q >= T + 2:
                    a.wait_ge(s_own, q - T - 1)
                nc.scalar.activation(blk[q % 2][:, :, :].rearrange("p t n -> p (t n)"), ptb[q % 2][:, 0:NP], ACT.Copy).then_inc(s_blk, 1)

        @b.tensor
        def _(pe):
            for q in range(2 * T):
                pe.wait_ge(s_sum, q + 1)
                if q >= 2:
                    pe.wait_ge(s_blk, q - 1)
                for j in range(T):
                    m = nc.tensor.transpose(ptb[q % 2][:, j * P:(j + 1) * P], g[0][buf(q)][:, j * P:(j + 1) * P], k.identb[:, :])
                m.then_inc(s_tr, 1)

        @b.sync
        def _(sp):
            sp.dma_start(iota[:, :], k.ins["c_iota"]).then_inc(s_i, 16)
            for q in range(2 * T):
                i = q % T
                if q >= T:
                    sp.wait_ge(s_sum, q + 1)
                    sp.dma_start(k.TB[n][:, :, i, :].rearrange("t p c -> p t c"), g[0][buf(q)][:, :].rearrange("p (t c) -> p t c", c=P)).then_inc(s_rt[i % 2], 16)
                if q < T or both:
                    sp.wait_ge(s_blk, q + 1)
                    to = segs[i] if q < T else k.Drow[n][0:NP, :].rearrange("(j p) (i c) -> i p j c", p=P, c=P)[i]
                    sp.dma_start(to, blk[q % 2][:, :, :]).then_inc(s_w[q % 2], 16)
            for u in range(2):
                sp.wait_ge(s_rt[u], 16 * ((T + 1 - u) // 2))
                sp.wait_ge(s_w[u], 16 * stored(2 * T - 2 + u))


def norm_gate(k, tag, xin, gamma, beta, hin, out):
    nc = k.nc
    with Phase(nc, tag) as f:
        x, sq, h = f.sb("x", [P, T, C], F32), f.sb("sq", [P, T, C], F32), f.sb("h", [P, T, C], F32)
        mu, var, eps = f.sb("mu", [P, T], F32), f.sb("var", [P, T], F32), f.sb("eps", [P, 1], F32)
        gb = f.sb("gb", [P, 2, C], F32)
        loaded, s_var, s_std, s_done, wrote = f.sem("in"), f.sem("var"), f.sem("std"), f.sem("done"), f.sem("wr")
        b = f.block()

        @b.sync
        def _(sp):
            sp.dma_start(x[:, :, :], nodes(xin)).then_inc(loaded, 16)
            sp.dma_start(h[:, :, :], nodes(hin)).then_inc(loaded, 16)
            sp.dma_start(gb[:, 0, :], gamma.rearrange("(a n) -> a n", a=1).to_broadcast([P, C])).then_inc(loaded, 16)
            sp.dma_start(gb[:, 1, :], beta.rearrange("(a n) -> a n", a=1).to_broadcast([P, C])).then_inc(loaded, 16)
            sp.wait_ge(s_done, 1)
            sp.dma_start(nodes(out), sq[:, :, :]).then_inc(wrote, 16)
            sp.wait_ge(wrote, 16)

        @b.vector
        def _(v):
            def tt(out_, a, c, op):
                v.tensor_tensor(out_, a, c, op)
                v.drain()

            def wide(col):
                return col[:, :].unsqueeze(2).to_broadcast([P, T, C])
            v.memset(eps[:, :], 1e-5)
            v.wait_ge(loaded, 64)
            v.tensor_reduce(mu[:, :], x[:, :, :], AX.X, ALU.add)
            v.drain()
            v.tensor_scalar(mu[:, :], mu[:, :], 1.0 / C, None, ALU.mult)
            v.drain()
            tt(x[:, :, :], x[:, :, :], wide(mu), ALU.subtract)
            tt(sq[:, :, :], x[:, :, :], x[:, :, :], ALU.mult)
            v.tensor_reduce(var[:, :], sq[:, :, :], AX.X, ALU.add).then_inc(s_var, 1)
            v.wait_ge(s_std, 1)
            v.reciprocal(var[:, :], mu[:, :])
            v.drain()
            tt(sq[:, :, :], x[:, :, :], wide(var), ALU.mult)
            tt(sq[:, :, :], sq[:, :, :], gb[:, 0, :].unsqueeze(1).to_broadcast([P, T, C]), ALU.mult)
            tt(sq[:, :, :], sq[:, :, :], gb[:, 1, :].unsqueeze(1).to_broadcast([P, T, C]), ALU.add)
            v.scalar_tensor_tensor(sq[:, :, :], sq[:, :, :], 0.0, h[:, :, :], ALU.max, ALU.add).then_inc(s_done, 1)

        @b.scalar
        def _(a):
            a.wait_ge(s_var, 1)
            nc.scalar.activation(mu[:, :], var[:, :], ACT.Sqrt, bias=eps[:, 0:1], scale=1.0 / C).then_inc(s_std, 1)


def attention(k, hh, x3, out):
    nc = k.nc
    H = HEADS
    with Phase(nc, "gat") as f0:
        x = f0.sb("x", [P, T, H, HD + 1], F32)
        asrc, adst = f0.sb("asrc", [P, H, T], F32), f0.sb("adst", [P, H, T], F32)
        m = f0.sb("m", [P, H, T], F32)
        r1, r3 = f0.sb("r1", [P, H, T], F32), f0.sb("r3", [P, H, T], F32)
        with Phase(nc, "gatl") as f:
            xx, tmp = f.sb("xx", [P, T, C], F32), f.sb("tmp", [P, T, C], F32)
            att, flat = f.sb("att", [P, 2, C], F32), f.sb("flat", [H * T, P], F32)
            pt = f.ps("pt", [P, PB])
            loaded, s_a, s_t, s_c, wrote = [f.sem(n) for n in ("in", "a", "t", "c", "wr")]
            b = f.block()

            @b.sync
            def _(sp):
                sp.dma_start(xx[:, :, :], nodes(hh)).then_inc(loaded, 16)
                for i, w in enumerate((k.ins["L3_gnn_att_src"], k.ins["L3_gnn_att_dst"])):
                    sp.dma_start(att[:, i, :], w.rearrange("(a h) d -> a (h d)", a=1).to_broadcast([P, C])).then_inc(loaded, 16)
                sp.wait_ge(s_c, 1)
                sp.dma_start(k.grow[0].rearrange("h (t p) -> (h t) p", p=P), flat[:, :]).then_inc(wrote, 16)
                sp.wait_ge(wrote, 16)

            @b.vector
            def _(v):
                v.memset(x[:, :, :, :], 1.0)
                v.wait_ge(loaded, 48)
                v.drain()
                v.tensor_copy(x[:, :, :, 0:HD], xx[:, :, :].rearrange("p t (h d) -> p t h d", d=HD))
                for i, to in enumerate((asrc, adst)):
                    v.tensor_tensor(tmp[:, :, :], xx[:, :, :], att[:, i, :].unsqueeze(1).to_broadcast([P, T, C]), ALU.mult)
                    v.drain()
                    v.tensor_reduce(to[:, :, :].rearrange("p h t -> p t h"), tmp[:, :, :].rearrange("p t (h d) -> p t h d", d=HD), AX.X, ALU.add)
                    v.drain()
                v.sem_inc(s_a, 1)
                v.wait_ge(s_t, 1)
                v.tensor_copy(flat[:, :], pt[0:H * T, 0:P]).then_inc(s_c, 1)

            @b.tensor
            def _(pe):
                pe.wait_ge(s_a, 1)
                nc.tensor.transpose(pt[0:H * T, 0:P], asrc[:, :, :].rearrange("p h t -> p (h t)"), k.ident[:, :]).then_inc(s_t, 1)

        with Phase(nc, "gatm") as f:
            ab, row = f.sb("ab", [P, H, NP], F32), f.sb("row", [P, 2, NP], BF16)
            pen, junk, flat = f.sb("pen", [P, NP], F32), f.sb("junk", [P, NP], F32), f.sb("flat", [H * T, 2, P], F32)
            pt = f.ps("pt", [P, PB])
            loaded, s_row, s_u, s_a, s_t, s_c, wrote = [f.sem("in"), [f.sem("row0"), f.sem("row1")], *[f.sem(n) for n in ("u", "a", "t", "c", "wr")]]
            b = f.block()

            @b.sync
            def _(sp):
                for h in range(H):
                    sp.dma_start(ab[:, h, :], k.grow[0, h:h + 1, :].to_broadcast([P, NP])).then_inc(loaded, 16)
                for t in range(T):
                    if t >= 2:
                        sp.wait_ge(s_u, t - 1)
                    sp.dma_start(row[:, t % 2, :], k.Drow[0][t * P:(t + 1) * P, :]).then_inc(s_row[t % 2], 16)
                sp.wait_ge(s_c, 1)
                for i in range(2):
                    sp.dma_start(k.grow[1 + i].rearrange("h (t p) -> (h t) p", p=P), flat[:, i, :]).then_inc(wrote, 16)
                sp.wait_ge(wrote, 32)

            @b.vector
            def _(v):
                v.wait_ge(loaded, 16 * H)
                for t in range(T):
                    v.wait_ge(s_row[t % 2], 16 * (t // 2 + 1))
                    v.tensor_scalar(pen[:, :], row[:, t % 2, :], 0.5, NEG, ALU.is_lt, ALU.mult).then_inc(s_u, 1)
                    v.drain()
                    for h in range(H):
                        v.tensor_tensor_reduce(out=junk[:, :], in0=pen[:, :], in1=ab[:, h, :], scale=1.0, scalar=FAR,
                                               op0=ALU.add, op1=ALU.max, accum_out=m[:, h, t:t + 1])
                        v.drain()
                v.tensor_tensor(m[:, :, :], m[:, :, :], asrc[:, :, :], ALU.max)
                v.drain()
                v.tensor_tensor(m[:, :, :], m[:, :, :], adst[:, :, :], ALU.add)
                v.drain()
                v.scalar_tensor_tensor(m[:, :, :], m[:, :, :], 0.2, m[:, :, :], ALU.mult, ALU.max)
                v.drain()
                v.tensor_tensor(r1[:, :, :], adst[:, :, :], m[:, :, :], ALU.subtract)
                v.tensor_scalar(r3[:, :, :], m[:, :, :], -0.8, None, ALU.mult).then_inc(s_a, 1)
                v.wait_ge(s_t, 1)
                v.tensor_copy(flat[:, :, :].rearrange("q i p -> q (i p)"), pt[0:H * T, 0:2 * P]).then_inc(s_c, 1)

            @b.tensor
            def _(pe):
                pe.wait_ge(s_a, 1)
                nc.tensor.transpose(pt[0:H * T, 0:P], r1[:, :, :].rearrange("p h t -> p (h t)"), k.ident[:, :])
                nc.tensor.transpose(pt[0:H * T, P:2 * P], r3[:, :, :].rearrange("p h t -> p (h t)"), k.ident[:, :]).then_inc(s_t, 1)

        with Phase(nc, "gate") as f:
            U = 4
            rb = f.sb("rb", [P, 2, H, P], F32)
            rb2 = f.sb("rb2", [P, 2, H, P], F32)
            rbs = [rb, rb2]
            blk = f.sb("blk", [P, 2, T, P], BF16)
            u = [f.sb(f"u{i}", [P, T, P], F32) for i in range(U)]
            w = [f.sb(f"w{i}", [P, T, P], F32) for i in range(2)]
            bb, o, e, inv, res = f.sb("bb", [P, C], F32), f.sb("o", [P, H, HD], F32), f.sb("e", [P, H, HD], F32), f.sb("inv", [P, H], F32), f.sb("res", [P, T, C], F32)
            po = [f.ps(f"po{i}", [P, PB]) for i in range(2)]
            loaded, s_b, s_u, s_w, s_e, s_p, s_mm, s_o, s_x, s_y, wrote = [f.sem("in"), [f.sem("b0"), f.sem("b1")],
                *[f.sem(n) for n in ("u", "w", "e", "p", "mm", "o", "x", "y", "wr")]]
            b = f.block()

            @b.sync
            def _(sp):
                sp.dma_start(bb[:, :], k.ins["L3_gnn_bias"].rearrange("(a n) -> a n", a=1).to_broadcast([P, C])).then_inc(loaded, 16)
                sp.dma_start(res[:, :, :], nodes(x3)).then_inc(loaded, 16)
                for t in range(T):
                    if t >= 2:
                        sp.wait_ge(s_p, H * (t - 1))
                    sp.dma_start(blk[:, t % 2, :, :], k.TB[0][t]).then_inc(s_b[t % 2], 16)
                    for i in range(2):
                        sp.dma_start(rbs[t % 2][:, i, :, :], k.grow[1 + i:2 + i, :, t * P:(t + 1) * P].to_broadcast([P, H, P])).then_inc(s_b[t % 2], 16)
                sp.wait_ge(s_o, T)
                sp.dma_start(nodes(out), res[:, :, :]).then_inc(wrote, 16)
                sp.wait_ge(wrote, 16)

            @b.gpsimd
            def _(pool):
                for t in range(T):
                    pool.wait_ge(s_b[t % 2], 48 * (t // 2 + 1))
                    for h in range(H):
                        q = t * H + h
                        if q >= U:
                            pool.wait_ge(s_mm, q - U + 1)
                        pool.tensor_tensor(u[q % U][:, :, :], asrc[:, h, :].unsqueeze(2).to_broadcast([P, T, P]),
                                           rbs[t % 2][:, 0, h, :].unsqueeze(1).to_broadcast([P, T, P]), ALU.add).then_inc(s_u, 1)

            @b.scalar
            def _(a):
                def elu(t):
                    a.wait_ge(s_x, t + 1)
                    nc.scalar.activation(e[:, :, :], e[:, :, :], ACT.Exp).then_inc(s_y, 1)
                for q in range(T * H):
                    a.wait_ge(s_w, q + 1)
                    nc.scalar.activation(w[q % 2][:, :, :], w[q % 2][:, :, :], ACT.Exp).then_inc(s_e, 1)
                    if q % H == 2 and q > H:
                        elu(q // H - 1)
                elu(T - 1)

            @b.vector
            def _(v):
                v.wait_ge(loaded, 32)

                def logits(q):
                    t, h = q // H, q % H
                    v.wait_ge(s_u, q + 1)
                    if h == 0:
                        v.wait_ge(s_b[t % 2], 48 * (t // 2 + 1))
                        v.tensor_tensor(blk[:, t % 2, t, :], blk[:, t % 2, t, :], k.identb[:, :], ALU.add)
                    if q >= 2:
                        v.wait_ge(s_p, q - 1)
                    v.scalar_tensor_tensor(w[q % 2][:, :, :], u[q % U][:, :, :], 0.2,
                                           rbs[t % 2][:, 1, h, :].unsqueeze(1).to_broadcast([P, T, P]), ALU.mult, ALU.add)
                    v.drain()
                    v.tensor_tensor(w[q % 2][:, :, :], w[q % 2][:, :, :], u[q % U][:, :, :], ALU.max).then_inc(s_w, 1)

                def weights(q):
                    v.wait_ge(s_e, q + 1)
                    v.scalar_tensor_tensor(u[q % U][:, :, :], w[q % 2][:, :, :], 1.0, blk[:, q // H % 2, :, :], ALU.min, ALU.mult).then_inc(s_p, 1)

                def finish(t):
                    v.wait_ge(s_mm, H * (t + 1))
                    src = po[t % 2][:, 0:H * (HD + 1)].rearrange("p (h d) -> p h d", h=H)
                    v.tensor_scalar(inv[:, :], src[:, :, HD], 1e-16, None, ALU.add)
                    v.drain()
                    v.reciprocal(inv[:, :], inv[:, :])
                    v.drain()
                    v.tensor_tensor(o[:, :, :], src[:, :, 0:HD], inv[:, :].unsqueeze(2).to_broadcast([P, H, HD]), ALU.mult)
                    v.drain()
                    v.tensor_tensor(o[:, :, :], o[:, :, :], bb[:, :].rearrange("p (h d) -> p h d", h=H), ALU.add)
                    v.drain()
                    v.tensor_scalar(e[:, :, :], o[:, :, :], 0.0, None, ALU.min).then_inc(s_x, 1)
                    v.scalar_tensor_tensor(res[:, t, :], o[:, :, :].rearrange("p h d -> p (h d)"), 0.0, res[:, t, :], ALU.max, ALU.add)

                def close(t):
                    v.wait_ge(s_y, t + 1)
                    v.drain()
                    v.scalar_tensor_tensor(res[:, t, :], e[:, :, :].rearrange("p h d -> p (h d)"), -1.0, res[:, t, :], ALU.add, ALU.add).then_inc(s_o, 1)
                for q in range(T * H):
                    logits(q)
                    if q:
                        weights(q - 1)
                    if q % H == 1 and q > H:
                        finish(q // H - 1)
                    if q % H == 3 and q > H:
                        close(q // H - 1)
                weights(T * H - 1)
                finish(T - 1)
                close(T - 1)

            @b.tensor
            def _(pe):
                for q in range(T * H):
                    t, h = q // H, q % H
                    pe.wait_ge(s_p, q + 1)
                    if h == 0 and t >= 2:
                        pe.wait_ge(s_o, t - 1)
                    for j in range(T):
                        mm = nc.tensor.matmul(po[t % 2][:, h * (HD + 1):(h + 1) * (HD + 1)], u[q % U][:, j, :], x[:, j, h, :], start=j == 0, stop=j == T - 1)
                    mm.then_inc(s_mm, 1)


SIZES = [(T,), (T * 3 // 5, T), (T // 3, T * 3 // 5, T)]


def first_level(k):
    nc = k.nc
    with Phase(nc, "first") as f:
        done = f.sem("done")
        b = f.block()

        @b.vector
        def _(v):
            v.memset(k.n[0][:, :], float(N))
            v.memset(k.runs[:, :], 1)
            v.drain()
            v.sem_inc(done, 1)
            v.wait_ge(done, 1)


def pool_level(k, l):
    nc = k.nc
    source_logits(k, l)
    softmax_sums(k, l)
    with ExitStack() as ctx:
        sb = lambda name, shape, dt: ctx.enter_context(nc.sbuf_tensor(f"{name}{l}", shape, dt))
        wa, wl = sb("wa", [P, T, K], BF16), sb("wl", [P, T, K], BF16)
        ta, tl = sb("ta", [P, 3, 2 * K], BF16), sb("tl", [P, 3, 2 * K], BF16)
        owna, ownl = sb("owna", [P, T], F32), sb("ownl", [P, T], F32)
        ranks(k, f"ranka{l}", k.ka, k.rows[0:1, :], wa, ta, owna)
        ranks(k, f"rankl{l}", k.kl, k.rows[1:2, :], wl, tl, ownl)
        match(k, l, wa, wl, ta, tl, ownl, SIZES[l])
    compact(k, l, SIZES[min(l + 1, DEPTH - 1)])
    pool_rows(k, l)
    coarsen(k, l)


def stages(k, sb):
    nc = k.nc
    load_constants(k)
    with ExitStack() as ctx:
        k.Tm = ctx.enter_context(nc.sbuf_tensor("by_source", [P, T, NP], F8))
        k.D = ctx.enter_context(nc.sbuf_tensor("by_dest", [P, T, NP], F8))
        build_counts(k)
        first_level(k)
        normalise(k, "ln0", k.ins["x"], k.h0)
        project(k, "pre", [(k.h0, k.ins["L0_gnn_w_pre"])], k.ins["L0_gnn_b_pre"], k.Xc)
        aggregate(k, "up0", k.Xc, k.ins["L0_gnn_w_up0"], k.ins["L0_gnn_b_up0"], k.TB[0], k.X[0], deg=k.deg[0], relu=True)
        ups = [(k.ins["L0_gnn_w_up1"], k.ins["L0_gnn_b_up1"]), (k.ins["L0_gnn_w_up2"], k.ins["L0_gnn_b_up2"]), (k.ins["L0_gnn_w_up3"], k.ins["L0_gnn_b_up3"])]
        for l in range(DEPTH):
            pool_level(k, l)
            to = k.X[l + 1] if l + 1 < DEPTH else k.Xc
            aggregate(k, f"up{l + 1}", k.Xc, *ups[l], k.TB[l + 1], to, deg=k.deg[l + 1], relu=True)
    downs = [(k.ins["L0_gnn_w_down0"], k.ins["L0_gnn_b_down0"]), (k.ins["L0_gnn_w_down1"], k.ins["L0_gnn_b_down1"]), (k.ins["L0_gnn_w_down2"], k.ins["L0_gnn_b_down2"])]
    for l in reversed(range(DEPTH)):
        unpool_rows(k, l)
        aggregate(k, f"down{l}", k.Xc, *downs[l], k.TB[l], k.Xc, deg=k.deg[l], relu=l > 0)
    x1, x2, x3 = k.X
    normalise(k, "ln1", k.ins["x"], k.h0, add=k.Xc, keep=x1)
    w1 = k.ins["L1_gnn_W1"]
    project(k, "mlp1", [(k.h0, w1[0:C, :]), (k.mean, w1[C:2 * C, :])], k.ins["L1_gnn_b1"], k.Xc, relu=True,
            shared=(k.ins["L1_gnn_u"][0, :], w1[2 * C:3 * C, :]))
    project(k, "mlp2", [(k.Xc, k.ins["L1_gnn_W2"])], k.ins["L1_gnn_b2"], k.Xc)
    normalise(k, "ln2", x1, k.h0, add=k.Xc, keep=x2)
    aggregate(k, "sage", k.h0, k.ins["L2_gnn_W_l"], k.ins["L2_gnn_b_l"], k.TB[0], k.Xc, w_own=k.ins["L2_gnn_W_r"])
    norm_gate(k, "lnq", k.Xc, k.ins["L2_gnn_gamma"], k.ins["L2_gnn_beta"], k.h0, k.Xc)
    normalise(k, "ln3", x2, k.h0, add=k.Xc, keep=x3)
    project(k, "proj", [(k.h0, k.ins["L3_gnn_W"])], None, k.Xc)
    attention(k, k.Xc, x3, k.out)


def constants():
    p = np.arange(P, dtype=np.float32)[:, None]
    node = p + P * np.arange(T, dtype=np.float32)[None, :]
    small = np.concatenate([
        node,
        np.where(node >= N, np.float32(FAR), np.float32(0)),
        np.broadcast_to(256.0 * (K - 1 - np.arange(K)), (P, K)),
        np.broadcast_to(K - 1.0 - np.arange(K), (P, K)),
        np.broadcast_to(G * np.arange(1.0, K + 1), (P, K)),
        np.broadcast_to(np.arange(T), (P, T)),
        p, EXP0 - 2 * p], 1).astype(np.float32)
    sel = np.zeros((T, T, P), np.float32)
    sel[np.arange(T), np.arange(T)] = 1
    return {"c_ident": np.eye(P, dtype=np.float32),
            "c_iota": np.broadcast_to(np.arange(NP, dtype=np.int16), (P, NP)).copy(),
            "c_small": small, "c_sel": sel.reshape(T, NP),
            "c_tri": np.triu(np.ones((P, P), np.float32), 1)}


S_ID, S_PAD, S_OFF, S_KK, S_GJ, S_T, S_P, S_CQ = 0, T, 2 * T, 2 * T + K, 2 * T + 2 * K, 2 * T + 3 * K, 3 * T + 3 * K, 3 * T + 3 * K + 1
S_N = 3 * T + 3 * K + 2


def laid_out(inputs):
    x = np.zeros((NP, C), inputs["x"].dtype)
    x[:N] = inputs["x"]
    edges = {}
    for name, fill in (("dst", ZERO + P), ("src", 0)):
        a = np.full(CH * P, fill, inputs[name].dtype)
        a[:E] = inputs[name]
        edges[f"{name}_T"] = np.ascontiguousarray(a.reshape(CH, P).T)
    attr = np.zeros((CH * P, C), inputs["edge_attr_128"].dtype)
    attr[:E] = inputs["edge_attr_128"]
    arrays = {"x": x, **edges, "edge_attr": attr, **constants()}
    for name, a in inputs.items():
        if name[:2] in ("L0", "L1", "L2", "L3"):
            arrays[name] = np.ascontiguousarray(a.T if name in ("L2_gnn_W_l", "L2_gnn_W_r") else a)
    return arrays


def build(nc, arrays):
    ios = {n: nc.dram_tensor(f"in_{n}", a.shape, mybir.dt.from_np(a.dtype), kind="ExternalInput").ap()
           for n, a in arrays.items()}
    k = Ctx(nc, ios)
    k.out = nc.dram_tensor("out", [NP, C], F32, kind="ExternalOutput").ap()
    dram = lambda name, shape, dt: nc.dram_tensor(name, shape, dt, kind="Internal").ap()
    k.Drow = [dram(f"Drow{l}", [NP + 1, NP], BF16) for l in range(DEPTH)]
    k.RT = dram("RT", [NP + 1, NP], BF16)
    k.TB = [dram(f"TB{l}", [T, P, T, P], BF16) for l in range(DEPTH + 1)]
    k.mean = dram("mean", [NP, C], F32)
    k.Xg = dram("Xg", [NP + 1, C], F32)
    k.X = [dram(f"X{l}", [NP, C], F32) for l in range(DEPTH)]
    k.Xc = dram("Xc", [NP, C], F32)
    k.h0 = dram("h0", [NP, C], F32)
    k.rows = dram("rows", [2, NP], F32)
    k.tab = dram("tab", [NP + 1, 4], F32)
    k.grow = dram("grow", [3, HEADS, NP], F32)
    with ExitStack() as ctx:
        sb = lambda name, shape, dt: ctx.enter_context(nc.sbuf_tensor(name, shape, dt))
        k.ident, k.identb = sb("ident", [P, P], F32), sb("identb", [P, P], BF16)
        k.ones = sb("ones", [P, P], F32)
        k.small = sb("small", [P, S_N], F32)
        k.count = sb("count", [P, T], F32)
        k.deg = [k.count] + [sb(f"deg{l}", [P, T], F32) for l in range(1, DEPTH + 1)]
        k.ss = [sb(f"ss{l}", [P, T], F32) for l in range(DEPTH)]
        k.cl = [sb(f"cl{l}", [P, T], I32) for l in range(DEPTH)]
        k.m1, k.m2, k.om = [sb(x, [P, T], I32) for x in ("m1", "m2", "om")]
        k.ka, k.kl = sb("ka", [P, T], F32), sb("kl", [P, T], F32)
        k.top, k.den = sb("top", [P, T], F32), sb("den", [P, T], F32)
        k.runs = sb("runs", [P, 4], I32)
        k.n = [sb(f"n{l}", [P, 1], F32) for l in range(DEPTH + 1)]
        stages(k, sb)


def kernel(**inputs):
    import concourse.bacc as bacc
    from concourse.bass_utils import run_bass_kernel_spmd

    arrays = laid_out({n: np.asarray(a) for n, a in inputs.items()})
    nc = bacc.Bacc("TRN2", target_bir_lowering=False, num_devices=1)
    build(nc, arrays)
    r = run_bass_kernel_spmd(nc, [{f"in_{n}": a for n, a in arrays.items()}], core_ids=[0])
    return np.asarray(r.results[0]["out"])[:N]
```
